# Optimizing a Trainium2 kernel written in Bass

```python
import numpy as np
import jax
import jax.numpy as jnp

def _softmax(x, axis=-1):
    return jax.nn.softmax(x, axis=axis)

def _gelu(x):
    return jax.nn.gelu(x, approximate=True)

def _silu(x):
    return jax.nn.silu(x)

def _sigmoid(x):
    return jax.nn.sigmoid(x)

def _layernorm(x, axis=-1, eps=1e-05):
    m = jnp.mean(x, axis=axis, keepdims=True)
    v = jnp.var(x, axis=axis, keepdims=True)
    return (x - m) / jnp.sqrt(v + eps)

def _scatter_add(tgt, idx, src, axis=0):
    return tgt.at[idx].add(src)

def _segment_sum(src, seg, n):
    return jax.ops.segment_sum(src, seg, n)
kernel_name = 'mk_macaron_d1_jaxref_r8_79d78f'

def setup_inputs(seed: int=0):
    np.random.seed(seed)
    _w = jnp.asarray

    def _L0_attn_setup():
        import jax, jax.numpy as jnp
        import numpy as np
        LN_EPS = 1e-05

        def _linear(x, w, b):
            return x @ w.T + b

        def _layernorm(x, g, b):
            mu = jnp.mean(x, axis=-1, keepdims=True)
            var = jnp.var(x, axis=-1, keepdims=True)
            return (x - mu) * jax.lax.rsqrt(var + LN_EPS) * g + b

        def _depthwise_conv1d(x, w):
            xc = jnp.swapaxes(x, 1, 2)
            y = jax.lax.conv_general_dilated(xc, w, window_strides=(1,), padding=[(1, 1)], dimension_numbers=('NCH', 'OIH', 'NCH'), feature_group_count=w.shape[0])
            return jnp.swapaxes(y, 1, 2)

        def _ssm(x, A, B, C):
            bsz = x.shape[0]
            h0 = jnp.zeros((bsz, A.shape[0]), dtype=x.dtype)

            def step(h, xt):
                h = h @ A.T + xt @ B.T
                return (h, h @ C.T)
            _, ys = jax.lax.scan(step, h0, jnp.swapaxes(x, 0, 1))
            return jnp.swapaxes(ys, 0, 1)
        key = jax.random.key(seed)
        d_model, d_state, expand = (128, 64, 2)
        B, S = (4, 256)
        ks = jax.random.split(key, 16)
        sm = 1.0 / np.sqrt(d_model)
        inp = {'x': jax.random.normal(ks[0], (B, S, d_model), jnp.float32), 'w1_w': jax.random.normal(ks[1], (d_model, d_model), jnp.float32) * sm, 'w1_b': jnp.zeros((d_model,), jnp.float32), 'v1_w': jax.random.normal(ks[2], (d_model, d_model), jnp.float32) * sm, 'v1_b': jnp.zeros((d_model,), jnp.float32), 'w2_w': jax.random.normal(ks[3], (d_model, d_model), jnp.float32) * sm, 'w2_b': jnp.zeros((d_model,), jnp.float32), 'conv_w': jax.random.normal(ks[4], (d_model, 1, 3), jnp.float32) * (1.0 / np.sqrt(3.0)), 'A': jax.random.normal(ks[5], (d_state, d_state), jnp.float32) * 0.05, 'Bm': jax.random.normal(ks[6], (d_state, d_model), jnp.float32) * sm, 'Cm': jax.random.normal(ks[7], (d_model, d_state), jnp.float32) * (1.0 / np.sqrt(d_state)), 'ln1_g': jnp.ones((d_model,), jnp.float32), 'ln1_b': jnp.zeros((d_model,), jnp.float32), 'ln2_g': jnp.ones((d_model,), jnp.float32), 'ln2_b': jnp.zeros((d_model,), jnp.float32), 'ff1_w': jax.random.normal(ks[8], (expand * d_model, d_model), jnp.float32) * sm, 'ff1_b': jnp.zeros((expand * d_model,), jnp.float32), 'ff2_w': jax.random.normal(ks[9], (d_model, expand * d_model), jnp.float32) * (1.0 / np.sqrt(expand * d_model)), 'ff2_b': jnp.zeros((d_model,), jnp.float32)}
        return inp
    _L0_attn_in = _L0_attn_setup()

    def _L0_ffn_setup():
        import jax, jax.numpy as jnp
        import numpy as np
        B, S, DIM = (4, 256, 128)
        E, K, HID = (8, 2, 512)
        key = jax.random.key(seed)
        ks = jax.random.split(key, 8)
        init = lambda k, sh: jax.random.normal(k, sh, jnp.float32) * 0.02
        return {'x': jax.random.normal(ks[0], (B, S, DIM), jnp.float32), 'gate_w': init(ks[1], (DIM, E)), 'gate_b': jnp.zeros((E,), jnp.float32), 'w1': init(ks[2], (E, DIM, HID)), 'b1': jnp.zeros((E, HID), jnp.float32), 'w2': init(ks[3], (E, HID, DIM)), 'b2': jnp.zeros((E, DIM), jnp.float32), 'ws1': init(ks[4], (DIM, HID)), 'bs1': jnp.zeros((HID,), jnp.float32), 'ws2': init(ks[5], (HID, DIM)), 'bs2': jnp.zeros((DIM,), jnp.float32)}
    _L0_ffn_in = _L0_ffn_setup()
    _d = {'L0_attn_x': _L0_attn_in['x'], 'L0_attn_w1_w': _L0_attn_in['w1_w'], 'L0_attn_w1_b': _L0_attn_in['w1_b'], 'L0_attn_v1_w': _L0_attn_in['v1_w'], 'L0_attn_v1_b': _L0_attn_in['v1_b'], 'L0_attn_w2_w': _L0_attn_in['w2_w'], 'L0_attn_w2_b': _L0_attn_in['w2_b'], 'L0_attn_conv_w': _L0_attn_in['conv_w'], 'L0_attn_A': _L0_attn_in['A'], 'L0_attn_Bm': _L0_attn_in['Bm'], 'L0_attn_Cm': _L0_attn_in['Cm'], 'L0_attn_ln1_g': _L0_attn_in['ln1_g'], 'L0_attn_ln1_b': _L0_attn_in['ln1_b'], 'L0_attn_ln2_g': _L0_attn_in['ln2_g'], 'L0_attn_ln2_b': _L0_attn_in['ln2_b'], 'L0_attn_ff1_w': _L0_attn_in['ff1_w'], 'L0_attn_ff1_b': _L0_attn_in['ff1_b'], 'L0_attn_ff2_w': _L0_attn_in['ff2_w'], 'L0_attn_ff2_b': _L0_attn_in['ff2_b'], 'L0_ffn_gate_w': _L0_ffn_in['gate_w'], 'L0_ffn_gate_b': _L0_ffn_in['gate_b'], 'L0_ffn_w1': _L0_ffn_in['w1'], 'L0_ffn_b1': _L0_ffn_in['b1'], 'L0_ffn_w2': _L0_ffn_in['w2'], 'L0_ffn_b2': _L0_ffn_in['b2'], 'L0_ffn_ws1': _L0_ffn_in['ws1'], 'L0_ffn_bs1': _L0_ffn_in['bs1'], 'L0_ffn_ws2': _L0_ffn_in['ws2'], 'L0_ffn_bs2': _L0_ffn_in['bs2']}
    _x0 = _d['L0_attn_x']
    _d['L0_attn_x'] = jax.random.normal(jax.random.fold_in(jax.random.key(seed), 1), (8, 512, 128), dtype=_x0.dtype)
    del _x0
    return _d

def reference(L0_attn_x, L0_attn_w1_w, L0_attn_w1_b, L0_attn_v1_w, L0_attn_v1_b, L0_attn_w2_w, L0_attn_w2_b, L0_attn_conv_w, L0_attn_A, L0_attn_Bm, L0_attn_Cm, L0_attn_ln1_g, L0_attn_ln1_b, L0_attn_ln2_g, L0_attn_ln2_b, L0_attn_ff1_w, L0_attn_ff1_b, L0_attn_ff2_w, L0_attn_ff2_b, L0_ffn_gate_w, L0_ffn_gate_b, L0_ffn_w1, L0_ffn_b1, L0_ffn_w2, L0_ffn_b2, L0_ffn_ws1, L0_ffn_bs1, L0_ffn_ws2, L0_ffn_bs2):

    def _L0_attn_ref(x, w1_w, w1_b, v1_w, v1_b, w2_w, w2_b, conv_w, A, Bm, Cm, ln1_g, ln1_b, ln2_g, ln2_b, ff1_w, ff1_b, ff2_w, ff2_b):
        import jax, jax.numpy as jnp
        import numpy as np
        LN_EPS = 1e-05

        def _linear(x, w, b):
            return x @ w.T + b

        def _layernorm(x, g, b):
            mu = jnp.mean(x, axis=-1, keepdims=True)
            var = jnp.var(x, axis=-1, keepdims=True)
            return (x - mu) * jax.lax.rsqrt(var + LN_EPS) * g + b

        def _depthwise_conv1d(x, w):
            xc = jnp.swapaxes(x, 1, 2)
            y = jax.lax.conv_general_dilated(xc, w, window_strides=(1,), padding=[(1, 1)], dimension_numbers=('NCH', 'OIH', 'NCH'), feature_group_count=w.shape[0])
            return jnp.swapaxes(y, 1, 2)

        def _ssm(x, A, B, C):
            bsz = x.shape[0]
            h0 = jnp.zeros((bsz, A.shape[0]), dtype=x.dtype)

            def step(h, xt):
                h = h @ A.T + xt @ B.T
                return (h, h @ C.T)
            _, ys = jax.lax.scan(step, h0, jnp.swapaxes(x, 0, 1))
            return jnp.swapaxes(ys, 0, 1)
        residual = x
        h = _layernorm(x, ln1_g, ln1_b)
        x1 = _linear(h, w1_w, w1_b)
        xc = jax.nn.silu(_depthwise_conv1d(x1, conv_w))
        x_ssm = _ssm(xc, A, Bm, Cm)
        v = jax.nn.silu(_linear(h, v1_w, v1_b))
        h = _linear(x_ssm * v, w2_w, w2_b)
        x = h + residual
        residual = x
        h = _layernorm(x, ln2_g, ln2_b)
        h = _linear(jax.nn.gelu(_linear(h, ff1_w, ff1_b), approximate=False), ff2_w, ff2_b)
        return h + residual

    def _L0_ffn_ref(x, gate_w, gate_b, w1, b1, w2, b2, ws1, bs1, ws2, bs2):
        import jax, jax.numpy as jnp
        import numpy as np
        B, S, DIM = (4, 256, 128)
        E, K, HID = (8, 2, 512)
        orig_shape = x.shape
        xf = x.reshape(-1, DIM)
        logits = xf @ gate_w + gate_b
        top_w, top_i = jax.lax.top_k(logits, K)
        gw = jax.nn.softmax(top_w, axis=-1).astype(xf.dtype)
        combine = (gw[:, :, None] * jax.nn.one_hot(top_i, E, dtype=xf.dtype)).sum(axis=1)
        out = jnp.zeros_like(xf)
        for e in range(E):
            h = jax.nn.gelu(xf @ w1[e] + b1[e], approximate=False)
            out = out + combine[:, e:e + 1] * (h @ w2[e] + b2[e])
        shared = jax.nn.gelu(xf @ ws1 + bs1, approximate=False) @ ws2 + bs2
        return (out + shared).reshape(orig_shape)
    x = L0_attn_x
    x = x + 0.5 * _L0_ffn_ref(_layernorm(x, axis=-1), L0_ffn_gate_w, L0_ffn_gate_b, L0_ffn_w1, L0_ffn_b1, L0_ffn_w2, L0_ffn_b2, L0_ffn_ws1, L0_ffn_bs1, L0_ffn_ws2, L0_ffn_bs2)
    x = x + _L0_attn_ref(_layernorm(x, axis=-1), L0_attn_w1_w, L0_attn_w1_b, L0_attn_v1_w, L0_attn_v1_b, L0_attn_w2_w, L0_attn_w2_b, L0_attn_conv_w, L0_attn_A, L0_attn_Bm, L0_attn_Cm, L0_attn_ln1_g, L0_attn_ln1_b, L0_attn_ln2_g, L0_attn_ln2_b, L0_attn_ff1_w, L0_attn_ff1_b, L0_attn_ff2_w, L0_attn_ff2_b)
    x = x + 0.5 * _L0_ffn_ref(_layernorm(x, axis=-1), L0_ffn_gate_w, L0_ffn_gate_b, L0_ffn_w1, L0_ffn_b1, L0_ffn_w2, L0_ffn_b2, L0_ffn_ws1, L0_ffn_bs1, L0_ffn_ws2, L0_ffn_bs2)
    return x

_drawn_inputs = setup_inputs


def setup_inputs(seed=0):
    import zlib

    import numpy as np

    out = dict(_drawn_inputs(seed))
    spreads = {'L0_attn_w1_b': (0.0, 0.31),
     'L0_attn_v1_b': (0.0, 0.331),
     'L0_attn_w2_b': (0.0, 0.1),
     'L0_attn_ln1_g': (1.0, 0.2),
     'L0_attn_ln1_b': (0.0, 0.1),
     'L0_attn_ln2_g': (1.0, 0.2),
     'L0_attn_ln2_b': (0.0, 0.1),
     'L0_attn_ff1_b': (0.0, 0.1),
     'L0_attn_ff2_b': (0.0, 0.1),
     'L0_ffn_gate_b': (0.0, 0.1),
     'L0_ffn_b1': (0.0, 0.678),
     'L0_ffn_b2': (0.0, 0.1),
     'L0_ffn_bs1': (0.0, 0.501),
     'L0_ffn_bs2': (0.0, 0.1)}
    factors = {}
    for name, (base, spread) in spreads.items():
        noise = np.random.default_rng([zlib.crc32(name.encode()), seed]).standard_normal(out[name].shape)
        drawn = base * np.exp(spread * noise) if base else spread * noise
        out[name] = jnp.asarray(drawn.astype(out[name].dtype))
    for name, factor in factors.items():
        out[name] = (out[name] * factor).astype(out[name].dtype)
    return out
```

```python
from contextlib import ExitStack

import numpy as np
import concourse.bass as bass
from concourse import mybir

F32 = mybir.dt.float32
F32R = mybir.dt.float32r
ALU = mybir.AluOpType
ACT = mybir.ActivationFunctionType
AX = mybir.AxisListType

P = 128
TW = 512
SUB = TW // P
EPS = 1e-5
NEG = -3.0e38
CH = 16


def macaron_kernel(nc, x, w1_w, w1_b, v1_w, v1_b, w2_w, w2_b, conv_w, A, Bm, Cm, ln1_g, ln1_b, ln2_g, ln2_b,
                   ff1_w, ff1_b, ff2_w, ff2_b, gate_w, gate_b, ew1, eb1, ew2, eb2, sw1, sb1, sw2, sb2, out):
    NB, TS, D = x.shape
    E, _, HID = ew1.shape
    HC = HID // P
    NT = NB * TS // TW
    NS = NT * SUB
    NST = A.shape[0]
    HB = NT // 2
    assert D == P and TS == TW and NST * 2 == P and E * (NS // 2) == P

    x_view = x.rearrange("b (s p) d -> p (b s) d", p=P)
    out_view = out.rearrange("b (s p) d -> p (b s) d", p=P)

    cols, n_rows, row_loads = {}, 0, []
    for name, ap, n in (("b1", sb1.rearrange("(c p) -> c p", p=P), HC), ("eb1", eb1.rearrange("e (c p) -> (e c) p", p=P), E * HC),
                        ("b2", sb2, 1), ("eb2", eb2, E), ("w1_b", w1_b, 1),
                        ("v1_b", v1_b, 1), ("w2_b", w2_b, 1), ("ln1_g", ln1_g, 1), ("ln1_b", ln1_b, 1),
                        ("ln2_g", ln2_g, 1), ("ln2_b", ln2_b, 1), ("ff1_b", ff1_b.rearrange("(c p) -> c p", p=P), 2),
                        ("ff2_b", ff2_b, 1)):
        if len(ap.shape) == 1:
            ap = ap.rearrange("(a p) -> a p", a=1)
        cols[name] = n_rows
        row_loads.append((n_rows, n, ap))
        n_rows += n

    comb_dram = [nc.dram_tensor(f"comb{f}_dram", (NS, E, P), F32).ap() for f in range(2)]

    with ExitStack() as ctx:
        def sb(name, shape, dt=F32):
            return ctx.enter_context(nc.sbuf_tensor(name, shape, dt))

        def sem(name):
            return ctx.enter_context(nc.semaphore(name))

        x_tok = sb("x_tok", [P, NS, D])
        acc = sb("acc", [P, NT * TW])
        res_tok = acc[:, :].rearrange("p (s d) -> p s d", d=D)
        xhi = sb("xhi", [P, NT * TW], F32R)
        xlo = sb("xlo", [P, NT * TW], F32R)
        combB = sb("combB", [P, 2, NT * TW])
        hf = sb("hf", [P, 2, HC, TW])
        hhi = sb("hhi", [P, 2, HC, TW], F32R)
        hlo = sb("hlo", [P, 2, HC, TW], F32R)
        wraw = sb("wraw", [P, 2, 2, HC * P])
        whi = sb("whi", [P, 2, 2, HC * P], F32R)
        wlo = sb("wlo", [P, 2, 2, HC * P], F32R)
        nrm = sb("nrm", [P, 2, SUB, P])
        nrmT = nrm[:, :, :, :].rearrange("p v s d -> p v (s d)")
        tmp = sb("tmp", [P, 2, TW])
        xf, ob = tmp, tmp
        stats = sb("stats", [P, NS, 6])
        mean = sb("mean", [P, NS])
        lnt = sb("lnt", [P, 5, NS])
        ve = sb("ve", [P, NS])
        rstd = sb("rstd", [P, NS])
        neghalf = sb("neghalf", [P, NS])
        rank = sb("rank", [P, E])
        gb = sb("gb", [P, E])
        gw = sb("gw", [P, E])
        r_ = {k: sb(f"rt_{k}", [P, NS, E]) for k in ("lg", "a", "b", "sel1", "sel2", "comb")}
        r1 = {k: sb(f"r1_{k}", [P, NS]) for k in ("m1", "m2", "k1", "k2", "d", "ex", "s", "wa", "wb")}
        cT = sb("cT", [P, 2, P])
        ident = sb("ident", [P, P])
        rows = sb("rows", [P, P])
        colv = sb("colv", [P, n_rows])
        cw = sb("cw", [P, 3])
        x1p = sb("x1p", [P, 2, TW + 2])
        wT = sb("wT", [P, 9, P])
        pw = sb("pw", [P, 9, P])
        pwT = sb("pwT", [P, 9, P])

        H = [ctx.enter_context(nc.psum_tensor(f"H{c}", [P, TW], F32)) for c in range(HC)]
        Y = [ctx.enter_context(nc.psum_tensor(f"Y{c}", [P, TW], F32)) for c in range(2)]
        T = [ctx.enter_context(nc.psum_tensor(f"T{c}", [P, TW], F32)) for c in range(2)]

        def col(name, k=0):
            return colv[:, cols[name] + k:cols[name] + k + 1]

        s_x = sem("x_loaded")
        s_ld = sem("constants_loaded")
        s_zero = sem("constants_zeroed")
        s_abd = sem("A_blocks_loaded")
        s_id = sem("ident_ready")
        s_wT = sem("weights_transposed")
        s_wc = sem("weights_ready")
        s_pp = sem("power_squared")
        s_pw = sem("power_ready")
        s_out = sem("out_stored")
        s_own = sem("held")
        s_chain = sem("vector_chain")
        chain = [0]

        def link(ins):
            chain[0] += 1
            ins.then_inc(s_chain, 1)
            nc.vector.wait_ge(s_chain, chain[0])

        def need(eng, s, v):
            if not isinstance(v, int) or v > 0:
                eng.wait_ge(s, v)

        def hold(eng, s, v):
            if not isinstance(v, int) or v > 0:
                eng.wait_ge(s, v)
                eng.sem_inc(s_own, 1)

        def pairs(eng, body):
            body(0)
            with eng.Fori(1, NT // 2) as j:
                body(j)

        LN = [{n: sem(f"ln{k}_{n}") for n in ("stats", "aggr", "var", "rstd")} for k in range(5)]
        FN = ["nrm", "nrmT", "xf", "xhi", "xlo", "gates", "lg", "d", "ex", "comb", "combT", "cT", "cst", "wl0",
              "wl1", "cl0", "cl1", "hip", "w", "zero", "h", "gelu", "hhi", "split", "y", "yv", "acc", "ob", "obT", "xd"]
        FS = [{n: sem(f"ffn{f}_{n}") for n in FN} for f in range(2)]
        GN = ["res", "nrm", "nrmT", "hT", "p1", "pv", "x1e", "vs", "c1", "c2", "cv", "xc", "pu", "ue", "sp", "sd", "hs", "py",
              "gm", "pw", "oe", "oT", "rd"]
        G = {n: sem(f"attn_{n}") for n in GN}
        KN = ["nrm", "nrmT", "hT", "f1", "ge", "f2", "oe", "oT", "xr", "xd"]
        K = {n: sem(f"ff_{n}") for n in KN}

        def slot(t):
            return bass.ds(t * SUB, SUB)

        def tile(t):
            return bass.ds(t * TW, TW)

        def ln_stats(src, k):
            S = LN[k]
            with nc.vector.Fori(0, NT) as t:
                for s in range(SUB):
                    nc.vector.bn_stats(stats[:, t * SUB + s, :], src[:, t * SUB + s, :]).then_inc(S["stats"], 1)
            nc.vector.wait_ge(S["stats"], NS)
            TT, TS = nc.vector.tensor_tensor, nc.vector.tensor_scalar
            TT(lnt[:, 0], stats[:, :, 1], stats[:, :, 4], ALU.add).then_inc(S["aggr"], 1)
            TT(lnt[:, 1], stats[:, :, 1], stats[:, :, 4], ALU.subtract).then_inc(S["aggr"], 1)
            TT(lnt[:, 2], stats[:, :, 2], stats[:, :, 5], ALU.add).then_inc(S["aggr"], 1)
            nc.vector.wait_ge(S["aggr"], 2)
            TS(mean[:], lnt[:, 0], 0.5, None, ALU.mult).then_inc(S["aggr"], 1)
            TT(lnt[:, 3], lnt[:, 1], lnt[:, 1], ALU.mult).then_inc(S["aggr"], 1)
            nc.vector.wait_ge(S["aggr"], 3)
            TS(lnt[:, 4], lnt[:, 2], 1.0 / D, EPS, ALU.mult, ALU.add).then_inc(S["aggr"], 1)
            nc.vector.wait_ge(S["aggr"], 6)
            nc.vector.scalar_tensor_tensor(ve[:], lnt[:, 3], 0.25, lnt[:, 4], ALU.mult,
                                           ALU.add).then_inc(S["var"], 1)

        def ln_rstd(k):
            nc.gpsimd.wait_ge(LN[k]["var"], 1)
            nc.gpsimd.tensor_tensor(rstd[:], ve[:], neghalf[:], ALU.pow).then_inc(LN[k]["rstd"], 1)

        def normalise(dst, src, t, done):
            for s in range(SUB):
                i = t * SUB + s
                ins = nc.vector.tensor_scalar(dst[:, s, :], src[:, i, :], mean[:, bass.ds(i, 1)],
                                              rstd[:, bass.ds(i, 1)], ALU.subtract, ALU.mult)
            ins.then_inc(done, 1)

        def transpose_tile(bank, src, done):
            for s in range(SUB):
                ins = nc.tensor.transpose(bank[:, s * P:(s + 1) * P], src(s), ident[:])
            ins.then_inc(done, 1)

        NE = E + 1

        def ffn_sp(f):
            sp, S = nc.sync, FS[f]

            def load_w(n, par, a, b):
                need(sp, S["w"], n - 1)
                sp.dma_start(wraw[:, par, 0, :], a).then_inc(S[f"wl{par}"], 16)
                sp.dma_start(wraw[:, par, 1, :].rearrange("p (c d) -> p c d", d=D), b).then_inc(S[f"wl{par}"], 16)

            def load_comb(n, par):
                need(sp, S["yv"], (n - 1) * NT)
                src = comb_dram[f][:, bass.ds(n - 1, 1), :].rearrange("s e p -> e s p").to_broadcast([P, NS, P])
                sp.dma_start(combB[:, par, :].rearrange("q (s p) -> q s p", p=P), src).then_inc(S[f"cl{par}"], 16)

            def expert_w(n, par):
                load_w(n, par, ew1[bass.ds(n - 1, 1)].rearrange("a d h -> (a d) h"),
                       ew2[bass.ds(n - 1, 1)].rearrange("a (c p) d -> p (a c) d", p=P))

            if f:
                sp.wait_ge(FS[0]["w"], NE)
            load_w(0, 0, sw1, sw2.rearrange("(c p) d -> p c d", p=P))
            expert_w(1, 1)
            for h in range(2):
                sp.wait_ge(S["cT"], h + 1)
                sp.dma_start(comb_dram[f][h * (NS // 2):(h + 1) * (NS // 2)].rearrange("s e p -> (s e) p"),
                             cT[:, h, :]).then_inc(S["cst"], 16)
            sp.wait_ge(S["cst"], 32)
            if f:
                sp.wait_ge(K["xd"], NT)
            load_comb(1, 1)
            expert_w(2, 0)
            load_comb(2, 0)
            with sp.Fori(1, E // 2) as i:
                for u in (1, 0):
                    n = i * 2 + (2 - u)
                    expert_w(n, u)
                    load_comb(n, u)

        def ffn_pool(f):
            pool, S = nc.gpsimd, FS[f]
            if f:
                pool.wait_ge(K["xd"], NT)
            pool.memset(combB[:, 0, :], 1.0).then_inc(S["zero"], 1)
            pool.memset(acc[:], 0.0).then_inc(S["zero"], 1)
            ln_rstd(4 * f)

            def split_w(n, par, k):
                hold(pool, S[f"wl{par}"], 32 * (k + 1))
                hold(pool, S["y"], (n - 1) * NT)
                nc.gpsimd.tensor_copy(whi[:, par], wraw[:, par]).then_inc(S["hip"], 1)
                pool.wait_ge(S["hip"], n + 1)
                nc.gpsimd.tensor_tensor(wlo[:, par], wraw[:, par], whi[:, par].bitcast(F32),
                                        ALU.subtract).then_inc(S["w"], 1)

            split_w(0, 0, 0)

            def lo_pair(j):
                for v in range(2):
                    t = j * 2 + v
                    pool.wait_ge(S["xhi"], t + 1)
                    nc.gpsimd.tensor_tensor(xlo[:, tile(t)], xf[:, v], xhi[:, tile(t)].bitcast(F32),
                                            ALU.subtract).then_inc(S["xlo"], 1)
            pairs(pool, lo_pair)

            def add(n, j):
                for v in range(2):
                    t = j * 2 + v
                    g = n * NT + t
                    pool.wait_ge(S["yv"], g + 1)
                    if isinstance(n, int) and n == 0:
                        pool.wait_ge(S["zero"], 2)
                    else:
                        pool.wait_ge(S["acc"], g - NT + 1)
                    nc.gpsimd.tensor_tensor(acc[:, tile(t)], acc[:, tile(t)], tmp[:, v],
                                            ALU.add).then_inc(S["acc"], 1)

            def adds(n):
                with pool.Fori(0, NT // 2) as j:
                    add(n, j)

            split_w(1, 1, 0)
            adds(0)
            with pool.Fori(0, E // 2 - 1) as i:
                split_w(i * 2 + 2, 0, i + 1)
                adds(i * 2 + 1)
                split_w(i * 2 + 3, 1, i + 1)
                adds(i * 2 + 2)
            split_w(NE - 1, 0, E // 2)
            adds(NE - 2)
            adds(NE - 1)

        def experts(eng, expert):
            expert(0, 0)
            with eng.Fori(0, E // 2) as i:
                expert(i * 2 + 1, 1)
                expert(i * 2 + 2, 0)

        def ffn_act(f):
            act, S = nc.scalar, FS[f]

            def pair(j):
                for v in range(2):
                    t = j * 2 + v
                    act.wait_ge(S["nrmT"], t + 1)
                    need(act, S["gates"], t - 1)
                    need(act, S["xlo"], t - 1)
                    nc.scalar.activation(xf[:, v], T[v][:], ACT.Copy).then_inc(S["xf"], 1)
                    nc.scalar.activation(xhi[:, tile(t)], T[v][:], ACT.Copy).then_inc(S["xhi"], 1)
            pairs(act, pair)
            act.wait_ge(S["d"], 1)
            nc.scalar.activation(r1["ex"][:], r1["d"][:], ACT.Exp).then_inc(S["ex"], 1)
            for h in range(2):
                act.wait_ge(S["combT"], h + 1)
                nc.scalar.activation(cT[:, h], T[h][:, 0:P], ACT.Copy).then_inc(S["cT"], 1)

            def gelu(n, t, v):
                g = n * NT + t
                need(act, S["split"], g - 1)
                for c in range(HC):
                    hold(act, S["h"], g * HC + c + 1)
                    b = colv[:, bass.ds(n * HC + (cols["b1"] + c), 1)]
                    nc.scalar.activation(hf[:, v, c], H[c][:], ACT.Gelu, bias=b).then_inc(S["gelu"], 1)

            def expert(n, par):
                gelu(n, 0, 0)
                gelu(n, 1, 1)
                with act.Fori(1, NT // 2) as j:
                    for v in range(2):
                        gelu(n, j * 2 + v, v)
            experts(act, expert)

            def back(j):
                for v in range(2):
                    t = j * 2 + v
                    hold(act, S["acc"], (NE - 1) * NT + t + 1)
                    hold(act, S["obT"], t - 1)
                    nc.scalar.activation(nrmT[:, v], acc[:, tile(t)], ACT.Copy, scale=0.5).then_inc(S["ob"], 1)
            pairs(act, back)

        def ffn_dve(f):
            dve, S = nc.vector, FS[f]
            if f == 0:
                dve.wait_ge(s_x, 16 * NT)
            else:
                dve.wait_ge(K["xd"], NT)
            ln_stats(x_tok, 4 * f)
            dve.wait_ge(LN[4 * f]["rstd"], 1)

            def pair(j):
                for v in range(2):
                    need(dve, S["nrmT"], j * 2 + v - 1)
                    normalise(nrm[:, v], x_tok, j * 2 + v, S["nrm"])
            pairs(dve, pair)

            dve.wait_ge(S["gates"], NT)
            dve.wait_ge(s_ld, 16 * N_LD)
            ex3 = lambda a: a[:].unsqueeze(2).to_broadcast([P, NS, E])
            tok3 = lambda a: a[:].unsqueeze(1).to_broadcast([P, NS, E])
            lg, ta, tb, s1, s2, comb = (r_[k] for k in ("lg", "a", "b", "sel1", "sel2", "comb"))
            TT, TR, STT = nc.vector.tensor_tensor, nc.vector.tensor_reduce, nc.vector.scalar_tensor_tensor
            link(TT(lg[:], Y[0][:, 0:NS * E].rearrange("p (s e) -> p s e", e=E), tok3(gb), ALU.add))
            dve.sem_inc(S["lg"], 1)

            def pick(src, m, key, sel):
                link(TR(m[:], src[:], AX.X, ALU.max))
                link(TT(ta[:], src[:], ex3(m), ALU.is_equal))
                link(TT(tb[:], ta[:], tok3(rank), ALU.mult))
                link(TR(key[:], tb[:], AX.X, ALU.max))
                link(TT(sel[:], tok3(rank), ex3(key), ALU.is_equal))
            pick(lg, r1["m1"], r1["k1"], s1)
            link(nc.vector.tensor_scalar(ta[:], s1[:], -1.0, 1.0, ALU.mult, ALU.add))
            link(TT(tb[:], lg[:], ta[:], ALU.mult))
            link(STT(lg[:], s1[:], NEG, tb[:], ALU.mult, ALU.add))
            pick(lg, r1["m2"], r1["k2"], s2)
            TT(r1["d"][:], r1["m2"][:], r1["m1"][:], ALU.subtract).then_inc(S["d"], 1)
            dve.wait_ge(S["ex"], 1)
            link(nc.vector.tensor_scalar_add(r1["s"][:], r1["ex"][:], 1.0))
            link(nc.vector.reciprocal(r1["wa"][:], r1["s"][:]))
            link(TT(r1["wb"][:], r1["ex"][:], r1["wa"][:], ALU.mult))
            link(TT(ta[:], s1[:], ex3(r1["wa"]), ALU.mult))
            link(TT(tb[:], s2[:], ex3(r1["wb"]), ALU.mult))
            TT(comb[:], ta[:], tb[:], ALU.add).then_inc(S["comb"], 1)

            def split(n, t, v):
                g = n * NT + t
                need(dve, S["y"], g - 1)
                for q in range(2):
                    cs = slice(q * HC // 2, (q + 1) * HC // 2)
                    dve.wait_ge(S["gelu"], g * HC + (q + 1) * HC // 2)
                    nc.vector.tensor_copy(hhi[:, v, cs], hf[:, v, cs]).then_inc(S["hhi"], 1)
                for q in range(2):
                    cs = slice(q * HC // 2, (q + 1) * HC // 2)
                    dve.wait_ge(S["hhi"], g * 2 + q + 1)
                    ins = TT(hlo[:, v, cs], hf[:, v, cs], hhi[:, v, cs].bitcast(F32), ALU.subtract)
                ins.then_inc(S["split"], 1)

            def weigh(n, t, v, par):
                g = n * NT + t
                dve.wait_ge(S["y"], g + 1)
                need(dve, S["acc"], g - 1)
                b = colv[:, bass.ds(n + cols["b2"], 1)]
                STT(tmp[:, v], Y[v][:], b, combB[:, par, tile(t)], ALU.add, ALU.mult).then_inc(S["yv"], 1)

            def expert(n, par):
                split(n, 0, 0)
                if not (isinstance(n, int) and n == 0):
                    weigh(n - 1, NT - 1, 1, 1 - par)
                if isinstance(n, int):
                    dve.wait_ge(S["zero"], 2)
                    dve.wait_ge(S["xlo"], NT)
                elif par:
                    dve.wait_ge(S["cl1"], (n + 1) * 8)
                else:
                    dve.wait_ge(S["cl0"], n * 8)
                split(n, 1, 1)
                weigh(n, 0, 0, par)
                with dve.Fori(1, NT // 2) as j:
                    split(n, j * 2, 0)
                    weigh(n, j * 2 - 1, 1, par)
                    split(n, j * 2 + 1, 1)
                    weigh(n, j * 2, 0, par)
            experts(dve, expert)
            weigh(NE - 1, NT - 1, 1, 0)

            def back(j):
                for v in range(2):
                    t = j * 2 + v
                    dve.wait_ge(S["obT"], t + 1)
                    xs = x_tok[:, slot(t), :]
                    TT(xs, xs, T[v][:].rearrange("p (s d) -> p s d", d=D), ALU.add).then_inc(S["xd"], 1)
            pairs(dve, back)

        def ffn_pe(f):
            pe, S = nc.tensor, FS[f]

            def pair(j):
                for v in range(2):
                    t = j * 2 + v
                    pe.wait_ge(S["nrm"], t + 1)
                    need(pe, S["xhi"], t - 1)
                    transpose_tile(T[v], lambda s: nrm[:, v, s, :], S["nrmT"])
                for v in range(2):
                    t = j * 2 + v
                    pe.wait_ge(S["xf"], t + 1)
                    for s in range(SUB):
                        ins = nc.tensor.matmul(Y[0][:, bass.ds((t * SUB + s) * E, E)], xf[:, v, s * P:(s + 1) * P],
                                               gw[:], start=True, stop=True)
                    ins.then_inc(S["gates"], 1)
            pairs(pe, pair)
            pe.wait_ge(S["xhi"], NT)

            def up(n, t, par):
                g = n * NT + t
                if isinstance(n, int):
                    pe.wait_ge(S["xlo"], t + 1)
                for c in range(HC):
                    need(pe, S["gelu"], (g - 1) * HC + c + 1)
                    ws = slice(c * P, (c + 1) * P)
                    nc.tensor.matmul(H[c][:], whi[:, par, 0, ws], xhi[:, tile(t)], start=True, stop=False)
                    nc.tensor.matmul(H[c][:], whi[:, par, 0, ws], xlo[:, tile(t)], start=False, stop=False)
                    nc.tensor.matmul(H[c][:], wlo[:, par, 0, ws], xhi[:, tile(t)], start=False,
                                     stop=True).then_inc(S["h"], 1)

            def down(n, t, v, par):
                g = n * NT + t
                pe.wait_ge(S["split"], g + 1)
                need(pe, S["yv"], g - 1)
                for c in range(HC):
                    ws = slice(c * P, (c + 1) * P)
                    nc.tensor.matmul(Y[v][:], whi[:, par, 1, ws], hhi[:, v, c], start=c == 0, stop=False)
                    nc.tensor.matmul(Y[v][:], whi[:, par, 1, ws], hlo[:, v, c], start=False, stop=False)
                    ins = nc.tensor.matmul(Y[v][:], wlo[:, par, 1, ws], hhi[:, v, c], start=False, stop=c == HC - 1)
                ins.then_inc(S["y"], 1)

            def expert(n, par):
                pe.wait_ge(S["w"], n + 1)
                up(n, 0, par)
                if not (isinstance(n, int) and n == 0):
                    down(n - 1, NT - 1, 1, 1 - par)
                else:
                    pe.wait_ge(S["lg"], 1)
                    pe.wait_ge(S["comb"], 1)
                    for h in range(2):
                        cs = r_["comb"][:, h * (NS // 2):(h + 1) * (NS // 2), :].rearrange("p s e -> p (s e)")
                        nc.tensor.transpose(T[h][:, 0:P], cs, ident[:]).then_inc(S["combT"], 1)
                up(n, 1, par)
                down(n, 0, 0, par)
                with pe.Fori(1, NT // 2) as j:
                    up(n, j * 2, par)
                    down(n, j * 2 - 1, 1, par)
                    up(n, j * 2 + 1, par)
                    down(n, j * 2, 0, par)
            experts(pe, expert)
            down(NE - 1, NT - 1, 1, 0)
            pe.wait_ge(S["cT"], 2)

            def back(j):
                for v in range(2):
                    t = j * 2 + v
                    pe.wait_ge(S["ob"], t + 1)
                    need(pe, S["xd"], t - 1)
                    transpose_tile(T[v], lambda s: nrm[:, v, s, :], S["obT"])
            pairs(pe, back)

        v_all = combB[:, 0, :]
        V = combB[:, 1, 0:HB * TW].rearrange("p (b t) -> p b t", t=TW)
        hT, cvb, xcb = hf[:, :, 0], hf[:, :, 1], hf[:, :, 2]
        hst = hf[:, 0, 3]
        BANKS = H

        def at(j, h):
            return j + HB * h

        def sweeps():
            L = CH.bit_length() - 1
            out_ = []
            for l in range(L):
                s = 1 << l
                out_.append((l, s - 1, 2 * s - 1, 2 * s, TW // (2 * s)))
            k = 1
            while k < TW // CH:
                out_.append((L + k.bit_length() - 1, CH - 1, CH - 1 + CH * k, CH, TW // CH - k))
                k *= 2
            for l in reversed(range(L)):
                s = 1 << l
                out_.append((l, 2 * s - 1, 3 * s - 1, 2 * s, TW // (2 * s) - 1))
            return out_

        def pieces(cnt):
            nb = max(1, min(HB, TW // cnt))
            return [(b, min(nb, HB - b)) for b in range(0, HB, nb)]

        def strided(b, nb, first, stride, cnt):
            return V[:, b:b + nb, first:first + stride * (cnt - 1) + 1:stride]

        def attn_dve():
            dve = nc.vector
            TT, STT = nc.vector.tensor_tensor, nc.vector.scalar_tensor_tensor
            dve.wait_ge(FS[0]["xd"], NT)
            ln_stats(x_tok, 1)
            dve.wait_ge(LN[1]["rstd"], 1)
            with dve.Fori(0, NT) as t:
                normalise(res_tok[:, slot(t), :], x_tok, t, G["res"])
            dve.wait_ge(G["res"], NT)
            ln_stats(res_tok, 2)
            dve.wait_ge(LN[2]["rstd"], 1)
            dve.wait_ge(s_ld, 16 * N_LD)

            def mix(j):
                for h in range(2):
                    need(dve, G["nrmT"], j * 2 + h - 1)
                    normalise(nrm[:, h], res_tok, at(j, h), G["nrm"])
                for h in range(2):
                    k = j * 2 + h
                    dve.wait_ge(G["x1e"], k + 1)
                    need(dve, G["xc"], k - 1)
                    nc.vector.tensor_scalar(cvb[:, h], x1p[:, h, 0:TW], cw[:, 0:1], None, ALU.mult).then_inc(G["c1"], 1)
                for i in (1, 2):
                    for h in range(2):
                        k = j * 2 + h
                        dve.wait_ge(G["c1" if i == 1 else "c2"], k + 1)
                        STT(cvb[:, h], x1p[:, h, i:i + TW], cw[:, i:i + 1], cvb[:, h], ALU.mult,
                            ALU.add).then_inc(G["c2" if i == 1 else "cv"], 1)
                for h in range(2):
                    dve.wait_ge(G["pu"], j * 2 + h + 1)
                    hs = slice(h * NST, (h + 1) * NST)
                    nc.vector.tensor_copy(combB[hs, 1, bass.ds(j * TW, TW)], Y[h][hs, :]).then_inc(G["ue"], 1)
            pairs(dve, mix)

            done = 0
            dve.wait_ge(G["ue"], NT)
            for n, (_, _, dst, st, cnt) in enumerate(sweeps()):
                for b, nb in pieces(cnt):
                    dve.wait_ge(G["sp"], done + 1)
                    v = strided(b, nb, dst, st, cnt)
                    TT(v, v, BANKS[done % 4][:, 0:nb * cnt].rearrange("p (b c) -> p b c", c=cnt),
                       ALU.add).then_inc(G["sd"], 1)
                    done += 1

            def gate(j):
                for h in range(2):
                    k = j * 2 + h
                    dve.wait_ge(G["py"], k + 1)
                    need(dve, G["pw"], k - 1)
                    TT(cvb[:, h], H[h][:], combB[:, 0, tile(at(j, h))], ALU.mult).then_inc(G["gm"], 1)
                for h in range(2):
                    dve.wait_ge(G["oT"], j * 2 + h + 1)
                    xs = res_tok[:, slot(at(j, h)), :]
                    TT(xs, xs, T[h][:].rearrange("p (s d) -> p s d", d=D), ALU.add).then_inc(G["rd"], 1)
            pairs(dve, gate)

            dve.wait_ge(G["rd"], NT)
            ln_stats(res_tok, 3)
            dve.wait_ge(LN[3]["rstd"], 1)

            def feed(j):
                for v in range(2):
                    need(dve, K["nrmT"], j * 2 + v - 1)
                    normalise(nrm[:, v], res_tok, j * 2 + v, K["nrm"])
                for v in range(2):
                    xs = x_tok[:, slot(j * 2 + v), :]
                    TT(xs, xs, res_tok[:, slot(j * 2 + v), :], ALU.add).then_inc(K["xr"], 1)
                for v in range(2):
                    t = j * 2 + v
                    dve.wait_ge(K["oT"], t + 1)
                    dve.wait_ge(K["xr"], t + 1)
                    xs = x_tok[:, slot(t), :]
                    TT(xs, xs, T[v][:].rearrange("p (s d) -> p s d", d=D), ALU.add).then_inc(K["xd"], 1)
            pairs(dve, feed)

        def attn_pool():
            for k in (1, 2, 3):
                ln_rstd(k)

        def attn_act():
            act = nc.scalar

            def mix(j):
                for h in range(2):
                    k = j * 2 + h
                    act.wait_ge(G["nrmT"], k + 1)
                    need(act, G["pv"], k - 1)
                    nc.scalar.activation(hT[:, h], T[h][:], ACT.Identity, scale=col("ln1_g"),
                                         bias=col("ln1_b")).then_inc(G["hT"], 1)
                for h in range(2):
                    k = j * 2 + h
                    act.wait_ge(G["p1"], k + 1)
                    need(act, G["cv"], k - 1)
                    nc.scalar.activation(x1p[:, h, 1:TW + 1], H[2 * h][:], ACT.Identity,
                                         bias=col("w1_b")).then_inc(G["x1e"], 1)
                    hold(act, G["pv"], k + 1)
                    nc.scalar.activation(combB[:, 0, tile(at(j, h))], H[2 * h + 1][:], ACT.Silu,
                                         bias=col("v1_b")).then_inc(G["vs"], 1)
                for h in range(2):
                    k = j * 2 + h
                    act.wait_ge(G["cv"], k + 1)
                    need(act, G["pu"], k - 1)
                    nc.scalar.activation(xcb[:, h], cvb[:, h], ACT.Silu).then_inc(G["xc"], 1)
            pairs(act, mix)

            act.wait_ge(G["sd"], N_SW)

            def gate(j):
                hold(act, G["py"], j * 2)
                nc.scalar.activation(hst, combB[:, 1, bass.ds(j * TW, TW)], ACT.Copy).then_inc(G["hs"], 1)
                for h in range(2):
                    k = j * 2 + h
                    act.wait_ge(G["pw"], k + 1)
                    need(act, G["oT"], k - 1)
                    nc.scalar.activation(ob[:, h], H[2 + h][:], ACT.Identity, bias=col("w2_b")).then_inc(G["oe"], 1)
            pairs(act, gate)

            def feed(j):
                for v in range(2):
                    t = j * 2 + v
                    act.wait_ge(K["nrmT"], t + 1)
                    need(act, K["f1"], (t - 1) * 2)
                    nc.scalar.activation(hT[:, v], T[v][:], ACT.Identity, scale=col("ln2_g"),
                                         bias=col("ln2_b")).then_inc(K["hT"], 1)
                for v in range(2):
                    t = j * 2 + v
                    need(act, K["f2"], t - 1)
                    for c in range(2):
                        act.wait_ge(K["f1"], t * 2 + c + 1)
                        nc.scalar.activation(hf[:, v, 1 + c], H[2 * v + c][:], ACT.Gelu,
                                             bias=col("ff1_b", c)).then_inc(K["ge"], 1)
                for v in range(2):
                    t = j * 2 + v
                    act.wait_ge(K["f2"], t + 1)
                    need(act, K["oT"], t - 1)
                    nc.scalar.activation(ob[:, v], Y[v][:], ACT.Identity, bias=col("ff2_b")).then_inc(K["oe"], 1)
            pairs(act, feed)

        def attn_pe():
            pe = nc.tensor
            MM = nc.tensor.matmul

            def mix(j):
                for h in range(2):
                    k = j * 2 + h
                    pe.wait_ge(G["nrm"], k + 1)
                    need(pe, G["hT"], k - 1)
                    transpose_tile(T[h], lambda s: nrm[:, h, s, :], G["nrmT"])
                for h in range(2):
                    k = j * 2 + h
                    pe.wait_ge(G["hT"], k + 1)
                    need(pe, G["x1e"], k - 1)
                    MM(H[2 * h][:], wT[:, W1], hT[:, h], start=True, stop=True).then_inc(G["p1"], 1)
                    need(pe, G["vs"], k - 1)
                    MM(H[2 * h + 1][:], wT[:, V1], hT[:, h], start=True, stop=True).then_inc(G["pv"], 1)
                for h in range(2):
                    k = j * 2 + h
                    pe.wait_ge(G["xc"], k + 1)
                    need(pe, G["ue"], k - 1)
                    MM(Y[h][h * NST:(h + 1) * NST, :], wT[:, BM, 0:NST], xcb[:, h], start=True,
                       stop=True).then_inc(G["pu"], 1)
            pairs(pe, mix)

            pe.wait_ge(G["vs"], NT)
            done = 0
            pe.wait_ge(G["ue"], NT)
            for n, (l, src, _, st, cnt) in enumerate(sweeps()):
                if done:
                    pe.wait_ge(G["sd"], done)
                for b, nb in pieces(cnt):
                    MM(BANKS[done % 4][:, 0:nb * cnt].rearrange("p (b c) -> p b c", c=cnt), pwT[:, l],
                       strided(b, nb, src, st, cnt), start=True, stop=True).then_inc(G["sp"], 1)
                    done += 1
            pe.wait_ge(G["sd"], done)

            def gate(j):
                pe.wait_ge(G["hs"], j + 1)
                for h in range(2):
                    k = j * 2 + h
                    need(pe, G["gm"], k - 1)
                    hs = slice(h * NST, (h + 1) * NST)
                    MM(H[h][:], wT[hs, CM, :], hst[hs, :], start=True, stop=True).then_inc(G["py"], 1)
                for h in range(2):
                    k = j * 2 + h
                    pe.wait_ge(G["gm"], k + 1)
                    need(pe, G["oe"], k - 1)
                    MM(H[2 + h][:], wT[:, W2], cvb[:, h], start=True, stop=True).then_inc(G["pw"], 1)
                for h in range(2):
                    k = j * 2 + h
                    pe.wait_ge(G["oe"], k + 1)
                    need(pe, G["rd"], k - 1)
                    transpose_tile(T[h], lambda s: ob[:, h, s * P:(s + 1) * P], G["oT"])
            pairs(pe, gate)

            pe.wait_ge(G["rd"], NT)

            def feed(j):
                for v in range(2):
                    t = j * 2 + v
                    pe.wait_ge(K["nrm"], t + 1)
                    need(pe, K["xd"], t - 1)
                    transpose_tile(T[v], lambda s: nrm[:, v, s, :], K["nrmT"])
                for v in range(2):
                    t = j * 2 + v
                    pe.wait_ge(K["hT"], t + 1)
                    need(pe, K["ge"], (t - 1) * 2)
                    for c in range(2):
                        MM(H[2 * v + c][:], wT[:, F1 + c], hT[:, v], start=True, stop=True).then_inc(K["f1"], 1)
                for v in range(2):
                    t = j * 2 + v
                    need(pe, K["oe"], t - 1)
                    for c in range(2):
                        pe.wait_ge(K["ge"], t * 2 + c + 1)
                        ins = MM(Y[v][:], wT[:, F2 + c], hf[:, v, 1 + c], start=c == 0, stop=c == 1)
                    ins.then_inc(K["f2"], 1)
                for v in range(2):
                    t = j * 2 + v
                    pe.wait_ge(K["oe"], t + 1)
                    transpose_tile(T[v], lambda s: ob[:, v, s * P:(s + 1) * P], K["oT"])
            pairs(pe, feed)

        N_SW = sum(len(pieces(cnt)) for _, _, _, _, cnt in sweeps())

        stage = hf[:, 0].rearrange("p c t -> p (c t)").rearrange("p (b d) -> p b d", d=P)
        W1, V1, W2, F1, F2, BM, CM = 0, 1, 2, 3, 5, 7, 8
        loads = [(stage[:, W1], w1_w), (stage[:, V1], v1_w), (stage[:, W2], w2_w),
                 (stage[:, F1:F1 + 2], ff1_w.rearrange("(c p) d -> p c d", p=P)),
                 (stage[:, F2:F2 + 2], ff2_w.rearrange("p (c d) -> p c d", d=P)),
                 (stage[0:NST, BM], Bm), (stage[:, CM, 0:NST], Cm), (stage[:, CM, NST:P], Cm),
                 (cw[:], conv_w.rearrange("d a k -> d (a k)")), (gw[:], gate_w),
                 (gb[:], gate_b.rearrange("(a e) -> a e", a=1).to_broadcast([P, E]))]
        loads += [(rows[r:r + n, :], ap) for r, n, ap in row_loads]
        N_LD = len(loads)
        SQ = 9
        block = ctx.enter_context(nc.Block())

        @block.sync
        def _(sp):
            for t in range(NT):
                sp.dma_start(x_tok[:, t * SUB:(t + 1) * SUB, :], x_view[:, t * SUB:(t + 1) * SUB, :]).then_inc(s_x, 16)
            for dst, src in loads:
                sp.dma_start(dst, src).then_inc(s_ld, 16)
            sp.wait_ge(s_zero, 1)
            for h in range(2):
                sp.dma_start(pw[h * NST:(h + 1) * NST, 0, h * NST:(h + 1) * NST], A).then_inc(s_abd, 16)
            ffn_sp(0)
            ffn_sp(1)
            with sp.Fori(0, NT) as t:
                sp.wait_ge(FS[1]["xd"], t + 1)
                sp.dma_start(out_view[:, slot(t), :], x_tok[:, slot(t), :]).then_inc(s_out, 16)
            sp.wait_ge(s_out, 16 * NT)

        @block.gpsimd
        def _(pool):
            pool.memset(pw[:, 0, :], 0.0).then_inc(s_zero, 1)
            pool.memset(ident[:], 0.0).then_inc(s_zero, 1)
            pool.memset(x1p[:], 0.0).then_inc(s_zero, 1)
            pool.memset(neghalf[:], -0.5).then_inc(s_zero, 1)
            for e in range(E):
                pool.memset(rank[:, e:e + 1], float(E - e)).then_inc(s_zero, 1)
            pool.wait_ge(s_zero, 4 + E)
            nc.gpsimd.affine_select(out=ident[:], in_=ident[:], compare_op=ALU.not_equal, fill=1.0, base=0,
                                    pattern=[[-1, P]], channel_multiplier=1).then_inc(s_id, 1)
            ffn_pool(0)
            attn_pool()
            ffn_pool(1)

        @block.scalar
        def _(act):
            for b in range(2):
                act.wait_ge(s_wT, b + 1)
                n = (4 if b == 0 else 3) * P + (0 if b == 0 else NST)
                nc.scalar.activation(wT[:, 4 * b:4 * b + 4].rearrange("p b d -> p (b d)")[:, 0:n], H[b][:, 0:n],
                                     ACT.Copy).then_inc(s_wc, 1)
            act.wait_ge(s_wT, 3)
            nc.scalar.activation(wT[:, CM], H[2][:, 0:P], ACT.Copy).then_inc(s_wc, 1)
            nc.scalar.activation(colv[:], H[2][:, P:P + n_rows], ACT.Copy).then_inc(s_wc, 1)
            nc.scalar.activation(pwT[:, 0], H[2][:, 2 * P:3 * P], ACT.Copy).then_inc(s_wc, 1)
            for l in range(1, SQ):
                act.wait_ge(s_pp, l)
                nc.scalar.activation(pw[:, l], H[3][:, 0:P], ACT.Copy).then_inc(s_pw, 1)
                nc.scalar.activation(pwT[:, l], H[3][:, P:2 * P], ACT.Copy).then_inc(s_pw, 1)
            ffn_act(0)
            attn_act()
            ffn_act(1)

        @block.vector
        def _(dve):
            ffn_dve(0)
            attn_dve()
            ffn_dve(1)

        @block.tensor
        def _(pe):
            pe.wait_ge(s_id, 1)
            pe.wait_ge(s_ld, 16 * N_LD)
            pe.wait_ge(s_abd, 32)
            TR = nc.tensor.transpose
            for b in range(7):
                ins = TR(H[b // 4][:, b % 4 * P:b % 4 * P + P], stage[:, b], ident[:])
                if b == 3:
                    ins.then_inc(s_wT, 1)
            TR(H[1][:, 3 * P:3 * P + NST], stage[0:NST, BM], ident[0:NST, 0:NST]).then_inc(s_wT, 1)
            TR(H[2][:, 0:P], stage[:, CM], ident[:])
            TR(H[2][:, P:P + n_rows], rows[0:n_rows, :], ident[0:n_rows, 0:n_rows])
            TR(H[2][:, 2 * P:3 * P], pw[:, 0], ident[:]).then_inc(s_wT, 1)
            pe.wait_ge(s_wc, 5)
            for l in range(1, SQ):
                if l > 1:
                    pe.wait_ge(s_pw, 2 * (l - 1))
                nc.tensor.matmul(H[3][:, 0:P], pwT[:, l - 1], pw[:, l - 1], start=True, stop=True)
                nc.tensor.matmul(H[3][:, P:2 * P], pw[:, l - 1], pwT[:, l - 1], start=True,
                                 stop=True).then_inc(s_pp, 1)
            pe.wait_ge(s_pw, 2 * (SQ - 1))
            ffn_pe(0)
            attn_pe()
            ffn_pe(1)


_INS = ['L0_attn_x', 'L0_attn_w1_w', 'L0_attn_w1_b', 'L0_attn_v1_w', 'L0_attn_v1_b', 'L0_attn_w2_w', 'L0_attn_w2_b',
        'L0_attn_conv_w', 'L0_attn_A', 'L0_attn_Bm', 'L0_attn_Cm', 'L0_attn_ln1_g', 'L0_attn_ln1_b', 'L0_attn_ln2_g',
        'L0_attn_ln2_b', 'L0_attn_ff1_w', 'L0_attn_ff1_b', 'L0_attn_ff2_w', 'L0_attn_ff2_b', 'L0_ffn_gate_w',
        'L0_ffn_gate_b', 'L0_ffn_w1', 'L0_ffn_b1', 'L0_ffn_w2', 'L0_ffn_b2', 'L0_ffn_ws1', 'L0_ffn_bs1', 'L0_ffn_ws2',
        'L0_ffn_bs2']
_OUTS = [((8, 512, 128), 'float32')]


def kernel(**inputs):
    import numpy as _np
    import concourse.bacc as _bacc
    from concourse import mybir as _mybir
    from concourse.bass_utils import run_bass_kernel_spmd as _run

    nc = _bacc.Bacc("TRN2", target_bir_lowering=False, num_devices=1)
    arrays, args = {}, []
    for name in _INS:
        a = _np.ascontiguousarray(inputs[name])
        arrays[f"in_{name}_dram"] = a
        args.append(nc.dram_tensor(f"in_{name}_dram", a.shape, _mybir.dt.from_np(a.dtype), kind="ExternalInput").ap())
    for i, (shape, dtype) in enumerate(_OUTS):
        dt = _mybir.dt.from_np(_np.dtype(dtype))
        args.append(nc.dram_tensor(f"out_{i}_dram", shape, dt, kind="ExternalOutput").ap())
    macaron_kernel(nc, *args)
    r = _run(nc, [arrays], core_ids=[0])
    got = tuple(r.results[0][f"out_{i}_dram"] for i in range(len(_OUTS)))
    return got[0]
```

```python
from contextlib import ExitStack

import numpy as np
import concourse.bass as bass
from concourse import mybir

F32 = mybir.dt.float32
F32R = mybir.dt.float32r
I32 = mybir.dt.int32
ALU = mybir.AluOpType
ACT = mybir.ActivationFunctionType
AX = mybir.AxisListType

P = 128
TW = 512
SUB = TW // P
BW = 256
SB = BW // P
EPS = 1e-5
NEG = -3.0e38
CH = 16
RSQRT_SEED = float(0x5F3759DF)


def macaron_kernel(nc, x, w1_w, w1_b, v1_w, v1_b, w2_w, w2_b, conv_w, A, Bm, Cm, ln1_g, ln1_b, ln2_g, ln2_b,
                   ff1_w, ff1_b, ff2_w, ff2_b, gate_w, gate_b, ew1, eb1, ew2, eb2, sw1, sb1, sw2, sb2, out):
    NB, TS, D = x.shape
    E, _, HID = ew1.shape
    HC = HID // P
    WC = HC * P
    NT = NB * TS // TW
    NS = NT * SUB
    HS = NS // 2
    NST = A.shape[0]
    HB = NT // 2
    HALF_BLOCKS = (2 * HS * P - E) // BW + E
    NBLK = 2 * HALF_BLOCKS
    SHBLK = NS // SB
    assert D == P and TS == TW and NST * 2 == P and HS * E == P

    x_view = x.rearrange("b (s p) d -> p (b s) d", p=P)
    out_view = out.rearrange("b (s p) d -> p (b s) d", p=P)

    cols, n_rows, row_loads = {}, 0, []
    for name, ap, n in (("b1", sb1.rearrange("(c p) -> c p", p=P), HC), ("eb1", eb1.rearrange("e (c p) -> (e c) p", p=P), E * HC),
                        ("b2", sb2, 1), ("eb2", eb2, E), ("w1_b", w1_b, 1),
                        ("v1_b", v1_b, 1), ("w2_b", w2_b, 1), ("ln1_g", ln1_g, 1), ("ln1_b", ln1_b, 1),
                        ("ln2_g", ln2_g, 1), ("ln2_b", ln2_b, 1), ("ff1_b", ff1_b.rearrange("(c p) -> c p", p=P), 2),
                        ("ff2_b", ff2_b, 1)):
        if len(ap.shape) == 1:
            ap = ap.rearrange("(a p) -> a p", a=1)
        cols[name] = n_rows
        row_loads.append((n_rows, n, ap))
        n_rows += n

    xs_dram = nc.dram_tensor("sorted_x_dram", (NBLK * BW, D), F32).ap()
    ys_dram = nc.dram_tensor("sorted_y_dram", (NBLK * BW, D), F32).ap()

    with ExitStack() as ctx:
        def sb(name, shape, dt=F32, scope=ctx):
            return scope.enter_context(nc.sbuf_tensor(name, shape, dt))

        def sem(name):
            return ctx.enter_context(nc.semaphore(name))

        x_tok = sb("x_tok", [P, NS, D])
        W = sb("W", [P, E + 1, 4, WC], F32R)
        GB = sb("GB", [P, 2, HS, D])
        res_tok = GB[:, :, :, :].rearrange("p a s d -> p (a s) d")
        wstage = GB[:, 1].rearrange("p (u w) d -> p u (w d)", u=2)
        XA = sb("XA", [P, HS, D])
        XN = [XA[:, :, :], GB[:, 0]]
        stats = sb("stats", [P, NS, 6])
        mean = sb("mean", [P, NS])
        lnt = sb("lnt", [P, 5, NS])
        ve = sb("ve", [P, NS])
        rstd = sb("rstd", [P, NS])
        ident = sb("ident", [P, P])
        before = sb("before", [P, P])
        ones = sb("ones", [P, P])
        rows = sb("rows", [P, P])
        colv = sb("colv", [P, n_rows])
        cw = sb("cw", [P, 3])
        zrow = sb("zrow", [P, D])
        gb = sb("gb", [P, E])
        gw = sb("gw", [P, E])
        rank = sb("rank", [P, E])
        starts = sb("starts", [P, HALF_BLOCKS])
        lt, ta, tb, sel1, sel2 = (sb(f"route_{k}", [P, HS, E]) for k in ("logit", "a", "b", "sel1", "sel2"))
        m1, m2, k1, k2, dd, ex, sm = (sb(f"route_{k}", [P, HS]) for k in ("m1", "m2", "k1", "k2", "d", "ex", "sum"))
        wab = sb("wab", [P, 2, 2, HS])
        posf = sb("posf", [P, 2, HS])
        posI = sb("posI", [P, 2, 2, HS], I32)
        cntI = sb("cntI", [P, 2, E], I32)
        ends = sb("ends", [P, 3, E])
        cmp_ = sb("cmp", [1, HALF_BLOCKS, E])
        eidf = sb("eidf", [1, HALF_BLOCKS])
        eid = sb("eid", [1, NBLK], I32)
        wT = sb("wT", [P, 9, P])
        pwT = sb("pwT", [P, 9, P])
        pw = sb("pw", [P, 2, P])
        with ExitStack() as phase:
            w1r = sb("w1r", [P, 2, 2, WC], F32R, phase)
            w2r = sb("w2r", [P, 2, 2, WC], F32R, phase)
            hf = sb("hf", [P, 2, HC, BW], F32, phase)
            hhi = sb("hhi", [P, 2, HC, BW], F32R, phase)
            hlo = sb("hlo", [P, 2, HC, BW], F32R, phase)
            xfT = sb("xfT", [P, NS * P], F32, phase)
            xin = sb("xin", [P, 2, SB, D], F32, phase)
            xbhi = sb("xbhi", [P, 2, BW], F32R, phase)
            xblo = sb("xblo", [P, 2, BW], F32R, phase)
            yT = sb("yT", [P, 2, BW], F32, phase)
            yo = sb("yo", [P, 2, BW], F32, phase)
        with ExitStack() as phase:
            v_all = sb("v_all", [P, NT * TW], F32, phase)
            Vt = sb("Vt", [P, HB * TW], F32, phase)
            nrm = sb("nrm", [P, 2, SUB, P], F32, phase)
            hT = sb("hT", [P, 2, TW], F32, phase)
            cvb = sb("cvb", [P, 2, TW], F32, phase)
            xcb = sb("xcb", [P, 2, TW], F32, phase)
            gel = sb("gel", [P, 2, 2, TW], F32, phase)
            hst = sb("hst", [P, TW], F32, phase)
            ob = sb("ob", [P, 2, TW], F32, phase)
            x1p = sb("x1p", [P, 2, TW + 2], F32, phase)

        H = [ctx.enter_context(nc.psum_tensor(f"H{c}", [P, TW], F32)) for c in range(HC)]
        Y = [ctx.enter_context(nc.psum_tensor(f"Y{c}", [P, TW], F32)) for c in range(2)]
        T = [ctx.enter_context(nc.psum_tensor(f"T{c}", [P, TW], F32)) for c in range(2)]
        TX, TY = T

        def col(name, k=0):
            return colv[:, cols[name] + k:cols[name] + k + 1]

        s_x = [sem(f"x{h}_loaded") for h in range(2)]
        s_wst = [sem(f"expert_weights{u}_loaded") for u in range(2)]
        s_whi = sem("expert_weights_hi")
        s_wlo = sem("expert_weights_lo")
        s_zrow = sem("rows_zeroed")
        s_bord = sem("borders_zeroed")
        s_ld = sem("constants_loaded")
        s_zero = sem("constants_zeroed")
        s_abd = sem("A_blocks_loaded")
        s_id = sem("ident_ready")
        s_wT = sem("weights_transposed")
        s_wc = sem("weights_ready")
        s_pp = sem("power_squared")
        s_pw = sem("power_ready")
        s_out = sem("out_stored")
        s_own = sem("held")
        s_chain = sem("vector_chain")
        chain = [0]

        def link(ins):
            chain[0] += 1
            ins.then_inc(s_chain, 1)
            nc.vector.wait_ge(s_chain, chain[0])

        def count(ins):
            chain[0] += 1
            ins.then_inc(s_chain, 1)

        def need(eng, s, v):
            if not isinstance(v, int) or v > 0:
                eng.wait_ge(s, v)

        def hold(eng, s, v):
            if not isinstance(v, int) or v > 0:
                eng.wait_ge(s, v)
                eng.sem_inc(s_own, 1)

        def pairs(eng, body):
            body(0)
            with eng.Fori(1, NT // 2) as j:
                body(j)

        def pipeline(eng, n, step):
            for b in (-1, 0, 1):
                step(b, b % 2)
            inner = (n - 3) // 2
            with eng.Fori(1, 1 + inner) as j:
                for u in range(2):
                    step(j * 2 + u, u)
            for b in range(2 + 2 * inner, n + 2):
                step(b, b % 2)

        def exists(b, n):
            return not isinstance(b, int) or 0 <= b < n

        FN = ["nrm0", "nrm1", "nrmT", "xfT", "gates", "m", "pre", "d", "ex", "pos0", "pos1", "sc0", "sc1",
              "ga0", "ga1", "ga2", "ga3", "gb0", "gb1", "gb2", "gb3", "x2", "comb"]
        FS = [{n: sem(f"ffn{f}_{n}") for n in FN} for f in range(2)]
        BN = ["TX", "xhi", "xlo", "w1", "w2", "up", "gelu", "hhi", "split", "y", "yT", "TY", "yo", "in0", "in1",
              "st0", "st1"]
        BS = [[{n: sem(f"ffn{f}_{k}_{n}") for n in BN if k == "routed" or n not in ("w1", "w2", "in0", "in1", "st0", "st1")}
               for k in ("shared", "routed")] for f in range(2)]
        GN = ["res", "nrm", "nrmT", "hT", "p1", "pv", "x1e", "vs", "c1", "c2", "cv", "xc", "pu", "ue", "sp", "sd", "hs", "py",
              "gm", "pw", "oe", "oT", "rd"]
        G = {n: sem(f"attn_{n}") for n in GN}
        KN = ["nrm", "nrmT", "hT", "f1", "ge", "f2", "oe", "oT", "xr", "xd"]
        K = {n: sem(f"ff_{n}") for n in KN}

        def slot(t):
            return bass.ds(t * SUB, SUB)

        def tile(t):
            return bass.ds(t * TW, TW)

        def ln(src, lo=0, hi=None):
            hi = NS if hi is None else hi
            TT, TS, STT = nc.vector.tensor_tensor, nc.vector.tensor_scalar, nc.vector.scalar_tensor_tensor
            r = slice(lo, hi)
            with nc.vector.Fori(lo // SUB, hi // SUB) as t:
                for s in range(SUB):
                    nc.vector.bn_stats(stats[:, t * SUB + s, :], src(t * SUB + s)).then_inc(s_chain, 1)
            chain[0] += hi - lo
            nc.vector.wait_ge(s_chain, chain[0])
            count(TT(lnt[:, 0, r], stats[:, r, 1], stats[:, r, 4], ALU.add))
            count(TT(lnt[:, 1, r], stats[:, r, 1], stats[:, r, 4], ALU.subtract))
            link(TT(lnt[:, 2, r], stats[:, r, 2], stats[:, r, 5], ALU.add))
            count(TS(mean[:, r], lnt[:, 0, r], 0.5, None, ALU.mult))
            count(TT(lnt[:, 3, r], lnt[:, 1, r], lnt[:, 1, r], ALU.mult))
            link(TS(lnt[:, 4, r], lnt[:, 2, r], 1.0 / D, EPS, ALU.mult, ALU.add))
            link(STT(ve[:, r], lnt[:, 3, r], 0.25, lnt[:, 4, r], ALU.mult, ALU.add))
            y0, sq, vy = lnt[:, 0, r], lnt[:, 1, r], lnt[:, 2, r]
            link(TS(y0.bitcast(I32), ve[:, r].bitcast(I32), -0.5, RSQRT_SEED, ALU.mult, ALU.add))
            steps = 4
            for i in range(steps):
                link(TT(sq, y0, y0, ALU.mult))
                link(STT(vy, sq, -0.5, ve[:, r], ALU.mult, ALU.mult))
                link(STT(rstd[:, r] if i == steps - 1 else y0, vy, 1.5, y0, ALU.add, ALU.mult))

        def normalise(dst, src, t, done):
            for s in range(SUB):
                i = t * SUB + s
                ins = nc.vector.tensor_scalar(dst[:, s, :], src[:, i, :], mean[:, bass.ds(i, 1)],
                                              rstd[:, bass.ds(i, 1)], ALU.subtract, ALU.mult)
            ins.then_inc(done, 1)

        def transpose_tile(bank, src, done):
            for s in range(SUB):
                ins = nc.tensor.transpose(bank[:, s * P:(s + 1) * P], src(s), ident[:])
            ins.then_inc(done, 1)

        NE = E + 1

        def scattered(sp, f, h):
            sp.wait_ge(FS[f][f"sc{h}"], 16 * 2 * HS)

        def ffn_sp(f):
            sp, S = nc.sync, BS[f][1]

            def load(b, u):
                need(sp, S["TX"], b - 1)
                sp.dma_start(xin[:, u], xs_dram[bass.ds(b * BW, BW), :].rearrange("(s p) d -> p s d", p=P)
                             ).then_inc(S[f"in{u}"], 16)

            def span(lo, hi):
                while lo < hi and (lo < 2 or lo % 2):
                    load(lo, lo % 2)
                    lo += 1
                with sp.Fori(lo // 2, hi // 2) as j:
                    for u in range(2):
                        load(j * 2 + u, u)
                if hi % 2:
                    load(hi - 1, 0)

            scattered(sp, f, 0)
            span(0, HALF_BLOCKS)
            scattered(sp, f, 1)
            span(HALF_BLOCKS, NBLK)

        def ffn_pool(f):
            pool, S, B = nc.gpsimd, FS[f], BS[f][1]

            def rows_of(h, k, s):
                return bass.IndirectOffsetOnAxis(posI[:, h, k, s:s + 1], 0)

            def scatter(h):
                pool.wait_ge(s_zrow, 16 * 2)
                if f:
                    pool.wait_ge(BS[0][1]["in0"], 16 * (NBLK // 2))
                    pool.wait_ge(BS[0][1]["in1"], 16 * (NBLK // 2))
                pool.wait_ge(S[f"nrm{h}"], HS)
                pool.wait_ge(S[f"pos{h}"], 2)
                for s in range(HS):
                    for k in range(2):
                        pool.indirect_dma_start(xs_dram[:, :], rows_of(h, k, s), XN[h][:, s, :],
                                                None).then_inc(S[f"sc{h}"], 16)

            def gather(h):
                ends_ = (h + 1) * HALF_BLOCKS
                pool.wait_ge(B["st0"], 16 * ((ends_ + 1) // 2))
                pool.wait_ge(B["st1"], 16 * (ends_ // 2))
                for q in range(4):
                    if h:
                        pool.wait_ge(S["comb"], (q + 1) * HS // 4)
                    for s in range(q * HS // 4, (q + 1) * HS // 4):
                        for k in range(2):
                            pool.indirect_dma_start(GB[:, k, s, :], None, ys_dram[0:ends_ * BW, :],
                                                    rows_of(h, k, s)).then_inc(S[f"g{'ab'[h]}{q}"], 16)

            scatter(0)
            scatter(1)
            pool.wait_ge(S["sc1"], 16 * 2 * HS)
            gather(0)
            gather(1)

        def routed_act(f, S, shared, n):
            act = nc.scalar

            def step(b, u):
                v = 1 - u
                if exists(b + 1, n):
                    need(act, S["up"], b * HC if isinstance(b, int) else b * HC)
                    if shared:
                        hold(act, s_whi, 1)
                        nc.scalar.activation(xbhi[:, v], xfT[:, bass.ds((b + 1) * BW, BW)],
                                             ACT.Copy).then_inc(S["xhi"], 1)
                    else:
                        act.wait_ge(S["TX"], b + 2)
                        nc.scalar.activation(xbhi[:, v], TX[:, 0:BW], ACT.Copy).then_inc(S["xhi"], 1)
                if exists(b, n):
                    need(act, S["split"], b - 1)
                    e = None if shared else act.value_load(eid[0:1, bass.ds(b, 1)], min_val=1, max_val=E)
                    for c in range(HC):
                        hold(act, S["up"], b * HC + c + 1)
                        bias = col("b1", c) if shared else colv[:, bass.ds(e * HC + (cols["b1"] + c), 1)]
                        nc.scalar.activation(hf[:, u, c], H[c][:, 0:BW], ACT.Gelu, bias=bias).then_inc(S["gelu"], 1)
                if exists(b - 2, n) and not shared:
                    act.wait_ge(S["TY"], b - 1)
                    if not (isinstance(b, int) and b - 4 < 0):
                        act.wait_ge(S[f"st{u}"], st_count(b, u))
                    nc.scalar.activation(yo[:, u], TY[:, 0:BW], ACT.Copy).then_inc(S["yo"], 1)
                if exists(b - 1, n):
                    need(act, S["TY"], b - 2)
                    hold(act, S["y"], b)
                    if shared:
                        bias = col("b2")
                    else:
                        e2 = act.value_load(eid[0:1, bass.ds(b - 1, 1)], min_val=1, max_val=E)
                        bias = colv[:, bass.ds(e2 + cols["b2"], 1)]
                    nc.scalar.activation(yT[:, v], Y[v][:, 0:BW], ACT.Identity, bias=bias).then_inc(S["yT"], 1)
                if exists(b - 2, n) and not shared:
                    act.wait_ge(S["yo"], b - 1)
                    act.dma_start(ys_dram[bass.ds((b - 2) * BW, BW), :].rearrange("(s p) d -> p s d", p=P),
                                  yo[:, u].rearrange("p (s d) -> p s d", d=D)).then_inc(S[f"st{u}"], 16)
            pipeline(act, n, step)

        def st_count(b, u):
            return 16 * ((b - 4) // 2 + 1) if isinstance(b, int) else (b - (2 + u)) * 8

        def routed_dve(f, S, shared, n):
            dve = nc.vector
            TT = nc.vector.tensor_tensor

            def step(b, u):
                v = 1 - u
                if exists(b + 1, n):
                    if not shared:
                        e = dve.value_load(eid[0:1, bass.ds(b + 1, 1)], min_val=1, max_val=E)
                        need(dve, S["up"], b * HC)
                        nc.vector.tensor_copy(w1r[:, v].rearrange("p a w -> p (a w)"),
                                              W[:, e, 0:2].rearrange("p a w -> p (a w)").bitcast(F32)
                                              ).then_inc(S["w1"], 1)
                    else:
                        need(dve, S["up"], b * HC)
                    dve.wait_ge(S["xhi"], b + 2)
                    x32 = xfT[:, bass.ds((b + 1) * BW, BW)] if shared else TX[:, 0:BW]
                    TT(xblo[:, v], x32, xbhi[:, v].bitcast(F32), ALU.subtract).then_inc(S["xlo"], 1)
                if exists(b, n):
                    if not shared:
                        e = dve.value_load(eid[0:1, bass.ds(b, 1)], min_val=1, max_val=E)
                    need(dve, S["y"], b - 1)
                    if not shared:
                        nc.vector.tensor_copy(w2r[:, u].rearrange("p a w -> p (a w)"),
                                              W[:, e, 2:4].rearrange("p a w -> p (a w)").bitcast(F32)
                                              ).then_inc(S["w2"], 1)
                    dve.wait_ge(S["gelu"], b * HC + HC)
                    nc.vector.tensor_copy(hhi[:, u], hf[:, u]).then_inc(S["hhi"], 1)
                if exists(b - 2, n) and shared:
                    dve.wait_ge(S["TY"], b - 1)
                    xs = x_tok[:, bass.ds((b - 2) * SB, SB), :]
                    nc.vector.scalar_tensor_tensor(xs, TY[:, 0:BW].rearrange("p (s d) -> p s d", d=D), 0.5, xs,
                                                   ALU.mult, ALU.add).then_inc(S["yo"], 1)
                if exists(b, n):
                    dve.wait_ge(S["hhi"], b + 1)
                    TT(hlo[:, u], hf[:, u], hhi[:, u].bitcast(F32), ALU.subtract).then_inc(S["split"], 1)
            pipeline(dve, n, step)

        def routed_pe(f, S, shared, n):
            pe = nc.tensor
            MM = nc.tensor.matmul

            def step(b, u):
                v = 1 - u
                if exists(b + 1, n) and not shared:
                    pe.wait_ge(S[f"in{v}"], 16 * ((b + 1) // 2 + 1) if isinstance(b, int) else (b + (3 - v)) * 8)
                    need(pe, S["xlo"], b + 1)
                    for s in range(SB):
                        ins = nc.tensor.transpose(TX[:, s * P:(s + 1) * P], xin[:, v, s, :], ident[:])
                    ins.then_inc(S["TX"], 1)
                if exists(b, n):
                    whi, wlo = (W[:, 0, 0], W[:, 0, 1]) if shared else (w1r[:, u, 0], w1r[:, u, 1])
                    pe.wait_ge(S["xlo"], b + 1)
                    if not shared:
                        pe.wait_ge(S["w1"], b + 1)
                    for c in range(HC):
                        need(pe, S["gelu"], (b - 1) * HC + c + 1)
                        ws = slice(c * P, (c + 1) * P)
                        MM(H[c][:, 0:BW], whi[:, ws], xbhi[:, u], start=True, stop=False)
                        MM(H[c][:, 0:BW], whi[:, ws], xblo[:, u], start=False, stop=False)
                        MM(H[c][:, 0:BW], wlo[:, ws], xbhi[:, u], start=False, stop=True).then_inc(S["up"], 1)
                if exists(b - 2, n):
                    pe.wait_ge(S["yT"], b - 1)
                    need(pe, S["yo"], b - 2)
                    for s in range(SB):
                        ins = nc.tensor.transpose(TY[:, s * P:(s + 1) * P], yT[:, u, s * P:(s + 1) * P], ident[:])
                    ins.then_inc(S["TY"], 1)
                if exists(b - 1, n):
                    whi, wlo = (W[:, 0, 2], W[:, 0, 3]) if shared else (w2r[:, v, 0], w2r[:, v, 1])
                    pe.wait_ge(S["split"], b)
                    if not shared:
                        pe.wait_ge(S["w2"], b)
                    need(pe, S["yT"], b - 2)
                    for c in range(HC):
                        ws = slice(c * P, (c + 1) * P)
                        MM(Y[v][:, 0:BW], whi[:, ws], hhi[:, v, c], start=c == 0, stop=False)
                        MM(Y[v][:, 0:BW], whi[:, ws], hlo[:, v, c], start=False, stop=False)
                        ins = MM(Y[v][:, 0:BW], wlo[:, ws], hhi[:, v, c], start=False, stop=c == HC - 1)
                    ins.then_inc(S["y"], 1)
            pipeline(pe, n, step)

        def prepare_dve(f, h):
            dve, S = nc.vector, FS[f]
            if f == 0:
                dve.wait_ge(s_x[h], 16)
            ln(lambda i: x_tok[:, i, :], h * HS, (h + 1) * HS)
            if f == 0 and h == 0:
                dve.wait_ge(s_wT, 3)
            with dve.Fori(0, HS // SUB) as t:
                for s in range(SUB):
                    i = t * SUB + s
                    nc.vector.tensor_scalar(XN[h][:, i, :], x_tok[:, i + h * HS, :], mean[:, bass.ds(i + h * HS, 1)],
                                            rstd[:, bass.ds(i + h * HS, 1)], ALU.subtract,
                                            ALU.mult).then_inc(S[f"nrm{h}"], 1)

        def prepare_pe(f, h):
            pe, S = nc.tensor, FS[f]
            pe.wait_ge(S[f"nrm{h}"], HS)
            for t in range(HS // SUB):
                n = h * (HS // SUB) + t
                need(pe, S["xfT"], n - HC + 1)
                transpose_tile(H[t], lambda s: XN[h][:, t * SUB + s, :], S["nrmT"])
            for t in range(HS // SUB):
                n = h * (HS // SUB) + t
                pe.wait_ge(S["xfT"], n + 1)
                for s in range(SUB):
                    i = t * SUB + s
                    ins = nc.tensor.matmul(Y[h][:, i * E:(i + 1) * E], xfT[:, (h * HS + i) * P:(h * HS + i + 1) * P],
                                           gw[:], start=True, stop=True)
            ins.then_inc(S["gates"], 1)
            pe.wait_ge(S["m"], h + 1)
            ms = ta[:, :, :].rearrange("p s e -> p (s e)")
            nc.tensor.matmul(TX[:, 0:P], before[:], ms, start=True, stop=True)
            nc.tensor.matmul(TX[:, P:2 * P], ones[:], ms, start=True, stop=True).then_inc(S["pre"], 1)

        def prepare_act(f, h):
            act, S = nc.scalar, FS[f]
            for t in range(HS // SUB):
                n = h * (HS // SUB) + t
                act.wait_ge(S["nrmT"], n + 1)
                nc.scalar.activation(xfT[:, n * TW:(n + 1) * TW], H[t][:], ACT.Copy).then_inc(S["xfT"], 1)
            act.wait_ge(S["d"], h + 1)
            nc.scalar.activation(ex[:], dd[:], ACT.Exp).then_inc(S["ex"], 1)

        def route_dve(f, h):
            dve, S = nc.vector, FS[f]
            ex3 = lambda a: a.unsqueeze(2).to_broadcast([P, HS, E])
            tok3 = lambda a: a.unsqueeze(1).to_broadcast([P, HS, E])
            TT, TR, TS = nc.vector.tensor_tensor, nc.vector.tensor_reduce, nc.vector.tensor_scalar
            STT = nc.vector.scalar_tensor_tensor
            dve.wait_ge(S["gates"], h + 1)
            dve.wait_ge(s_ld, 16 * N_LD)
            link(TT(lt[:], Y[h][:, 0:P].rearrange("p (s e) -> p s e", e=E), tok3(gb[:]), ALU.add))

            def pick(m, key, sel):
                link(TR(m[:], lt[:], AX.X, ALU.max))
                link(TT(ta[:], lt[:], ex3(m[:]), ALU.is_equal))
                link(TT(tb[:], ta[:], tok3(rank[:]), ALU.mult))
                link(TR(key[:], tb[:], AX.X, ALU.max))
                link(TT(sel[:], tok3(rank[:]), ex3(key[:]), ALU.is_equal))
            pick(m1, k1, sel1)
            link(TS(ta[:], sel1[:], -1.0, 1.0, ALU.mult, ALU.add))
            link(TT(tb[:], lt[:], ta[:], ALU.mult))
            link(STT(lt[:], sel1[:], NEG, tb[:], ALU.mult, ALU.add))
            pick(m2, k2, sel2)
            TT(dd[:], m2[:], m1[:], ALU.subtract).then_inc(S["d"], 1)
            TT(ta[:], sel1[:], sel2[:], ALU.add).then_inc(S["m"], 1)
            dve.wait_ge(S["ex"], h + 1)
            link(TS(sm[:], ex[:], 1.0, None, ALU.add))
            link(nc.vector.reciprocal(m1[:], sm[:]))
            link(TT(m2[:], ex[:], m1[:], ALU.mult))
            TS(wab[:, h, 0], m1[:], 0.5, None, ALU.mult).then_inc(S["x2"], 1)
            TS(wab[:, h, 1], m2[:], 0.5, None, ALU.mult).then_inc(S["x2"], 1)
            dve.wait_ge(S["pre"], h + 1)
            pre = TX[:, 0:P].rearrange("p (s e) -> p s e", e=E)
            tot = TX[:, P:2 * P].rearrange("p (s e) -> p s e", e=E)
            for e in range(E):
                ins = nc.vector.tensor_tensor_scan(tb[:, :, e], ones[:, 0:HS], tot[:, :, e], 0.0, ALU.mult, ALU.add)
            link(ins)
            link(TS(cntI[:, 0], tb[:, HS - 1, :], float(BW - 1), None, ALU.add))
            link(TS(cntI[:, 1], cntI[:, 0], BW.bit_length() - 1, BW.bit_length() - 1, ALU.logical_shift_right,
                    ALU.logical_shift_left))
            link(nc.vector.tensor_copy(ends[:, 0], cntI[:, 1]))
            link(nc.vector.tensor_tensor_scan(ends[:, 1], ones[:, 0:E], ends[:, 0], 0.0, ALU.mult, ALU.add))
            link(TT(ends[:, 2], ends[:, 1], ends[:, 0], ALU.subtract))
            link(TT(ta[:], tb[:], tot, ALU.subtract))
            link(TT(tb[:], ta[:], pre, ALU.add))
            link(TT(ta[:], tb[:], tok3(ends[:, 2]), ALU.add))
            for k, sel in enumerate((sel1, sel2)):
                link(TT(tb[:], ta[:], sel[:], ALU.mult))
                link(TR(posf[:, k], tb[:], AX.X, ALU.add))
            TS(posI[:, h], posf[:], float(h * HALF_BLOCKS * BW), None, ALU.add).then_inc(S[f"pos{h}"], 1)
            NBH = [1, HALF_BLOCKS, E]
            link(TT(cmp_[:], starts[0:1, :].unsqueeze(2).to_broadcast(NBH), ends[0:1, 1].unsqueeze(1).to_broadcast(NBH),
                    ALU.is_ge))
            link(TR(eidf[:], cmp_[:], AX.X, ALU.add))
            TS(eid[0:1, h * HALF_BLOCKS:(h + 1) * HALF_BLOCKS], eidf[:], float(E - 1), 1.0, ALU.min,
               ALU.add).then_inc(S[f"pos{h}"], 1)

        def combine(f, h, after=None):
            dve, S = nc.vector, FS[f]
            for q in range(4):
                dve.wait_ge(S[f"g{'ab'[h]}{q}"], 16 * 2 * HS // 4)
                for k in range(2):
                    for s in range(q * HS // 4, (q + 1) * HS // 4):
                        xs = x_tok[:, h * HS + s, :]
                        if k:
                            dve.wait_ge(S["x2"], 4 + h * HS + s + 1)
                        nc.vector.scalar_tensor_tensor(xs, GB[:, k, s, :], wab[:, h, k, s:s + 1], xs, ALU.mult,
                                                       ALU.add).then_inc(S["comb" if k else "x2"], 1)

        def ffn_dve(f):
            prepare_dve(f, 0)
            route_dve(f, 0)
            if f == 0:
                nc.vector.wait_ge(s_wlo, 1)
            prepare_dve(f, 1)
            route_dve(f, 1)
            routed_dve(f, BS[f][0], True, SHBLK)
            nc.vector.wait_ge(s_wlo, NE)
            routed_dve(f, BS[f][1], False, NBLK)
            nc.vector.wait_ge(BS[f][0]["yo"], SHBLK)
            combine(f, 0)
            combine(f, 1)

        def ffn_act(f):
            routed_act(f, BS[f][0], True, SHBLK)
            for h in range(2):
                nc.scalar.wait_ge(FS[f][f"pos{h}"], 2)
            routed_act(f, BS[f][1], False, NBLK)

        def ffn_pe(f):
            prepare_pe(f, 0)
            prepare_pe(f, 1)
            nc.tensor.wait_ge(s_wlo, 1)
            routed_pe(f, BS[f][0], True, SHBLK)
            routed_pe(f, BS[f][1], False, NBLK)

        V = Vt[:, :].rearrange("p (b t) -> p b t", t=TW)
        BANKS = H

        def at(j, h):
            return j + HB * h

        def sweeps():
            L = CH.bit_length() - 1
            out_ = []
            for l in range(L):
                s = 1 << l
                out_.append((l, s - 1, 2 * s - 1, 2 * s, TW // (2 * s)))
            k = 1
            while k < TW // CH:
                out_.append((L + k.bit_length() - 1, CH - 1, CH - 1 + CH * k, CH, TW // CH - k))
                k *= 2
            for l in reversed(range(L)):
                s = 1 << l
                out_.append((l, 2 * s - 1, 3 * s - 1, 2 * s, TW // (2 * s) - 1))
            return out_

        def pieces(cnt):
            nb = max(1, min(HB, TW // cnt))
            return [(b, min(nb, HB - b)) for b in range(0, HB, nb)]

        def strided(b, nb, first, stride, cnt):
            return V[:, b:b + nb, first:first + stride * (cnt - 1) + 1:stride]

        def attn_dve():
            dve = nc.vector
            TT, STT = nc.vector.tensor_tensor, nc.vector.scalar_tensor_tensor
            dve.wait_ge(FS[0]["comb"], NS)
            ln(lambda i: x_tok[:, i, :])
            with dve.Fori(0, NT) as t:
                normalise(res_tok[:, slot(t), :], x_tok, t, G["res"])
            dve.wait_ge(G["res"], NT)
            ln(lambda i: res_tok[:, i, :])
            dve.wait_ge(s_ld, 16 * N_LD)

            def mix(j):
                for h in range(2):
                    need(dve, G["nrmT"], j * 2 + h - 1)
                    normalise(nrm[:, h], res_tok, at(j, h), G["nrm"])
                for h in range(2):
                    k = j * 2 + h
                    dve.wait_ge(G["x1e"], k + 1)
                    need(dve, G["xc"], k - 1)
                    nc.vector.tensor_scalar(cvb[:, h], x1p[:, h, 0:TW], cw[:, 0:1], None, ALU.mult).then_inc(G["c1"], 1)
                for i in (1, 2):
                    for h in range(2):
                        k = j * 2 + h
                        dve.wait_ge(G["c1" if i == 1 else "c2"], k + 1)
                        STT(cvb[:, h], x1p[:, h, i:i + TW], cw[:, i:i + 1], cvb[:, h], ALU.mult,
                            ALU.add).then_inc(G["c2" if i == 1 else "cv"], 1)
                for h in range(2):
                    dve.wait_ge(G["pu"], j * 2 + h + 1)
                    hs = slice(h * NST, (h + 1) * NST)
                    nc.vector.tensor_copy(Vt[hs, bass.ds(j * TW, TW)], Y[h][hs, :]).then_inc(G["ue"], 1)
            pairs(dve, mix)

            done = 0
            dve.wait_ge(G["ue"], NT)
            for n, (_, _, dst, st, cnt) in enumerate(sweeps()):
                for b, nb in pieces(cnt):
                    dve.wait_ge(G["sp"], done + 1)
                    v = strided(b, nb, dst, st, cnt)
                    TT(v, v, BANKS[done % 4][:, 0:nb * cnt].rearrange("p (b c) -> p b c", c=cnt),
                       ALU.add).then_inc(G["sd"], 1)
                    done += 1

            def gate(j):
                for h in range(2):
                    k = j * 2 + h
                    dve.wait_ge(G["py"], k + 1)
                    need(dve, G["pw"], k - 1)
                    TT(cvb[:, h], H[h][:], v_all[:, tile(at(j, h))], ALU.mult).then_inc(G["gm"], 1)
                for h in range(2):
                    dve.wait_ge(G["oT"], j * 2 + h + 1)
                    xs = res_tok[:, slot(at(j, h)), :]
                    TT(xs, xs, T[h][:].rearrange("p (s d) -> p s d", d=D), ALU.add).then_inc(G["rd"], 1)
            pairs(dve, gate)

            dve.wait_ge(G["rd"], NT)
            ln(lambda i: res_tok[:, i, :])

            def feed(j):
                for v in range(2):
                    need(dve, K["nrmT"], j * 2 + v - 1)
                    normalise(nrm[:, v], res_tok, j * 2 + v, K["nrm"])
                for v in range(2):
                    xs = x_tok[:, slot(j * 2 + v), :]
                    TT(xs, xs, res_tok[:, slot(j * 2 + v), :], ALU.add).then_inc(K["xr"], 1)
                for v in range(2):
                    t = j * 2 + v
                    dve.wait_ge(K["oT"], t + 1)
                    dve.wait_ge(K["xr"], t + 1)
                    xs = x_tok[:, slot(t), :]
                    TT(xs, xs, T[v][:].rearrange("p (s d) -> p s d", d=D), ALU.add).then_inc(K["xd"], 1)
            pairs(dve, feed)

        def attn_pool():
            nc.gpsimd.wait_ge(BS[0][1]["yo"], NBLK)
            nc.gpsimd.memset(x1p[:], 0.0).then_inc(s_bord, 1)

        def attn_act():
            act = nc.scalar

            def mix(j):
                for h in range(2):
                    k = j * 2 + h
                    act.wait_ge(G["nrmT"], k + 1)
                    need(act, G["pv"], k - 1)
                    nc.scalar.activation(hT[:, h], T[h][:], ACT.Identity, scale=col("ln1_g"),
                                         bias=col("ln1_b")).then_inc(G["hT"], 1)
                for h in range(2):
                    k = j * 2 + h
                    act.wait_ge(G["p1"], k + 1)
                    need(act, G["cv"], k - 1)
                    if isinstance(k, int) and k == 0:
                        act.wait_ge(s_bord, 1)
                    nc.scalar.activation(x1p[:, h, 1:TW + 1], H[2 * h][:], ACT.Identity,
                                         bias=col("w1_b")).then_inc(G["x1e"], 1)
                    hold(act, G["pv"], k + 1)
                    nc.scalar.activation(v_all[:, tile(at(j, h))], H[2 * h + 1][:], ACT.Silu,
                                         bias=col("v1_b")).then_inc(G["vs"], 1)
                for h in range(2):
                    k = j * 2 + h
                    act.wait_ge(G["cv"], k + 1)
                    need(act, G["pu"], k - 1)
                    nc.scalar.activation(xcb[:, h], cvb[:, h], ACT.Silu).then_inc(G["xc"], 1)
            pairs(act, mix)

            act.wait_ge(G["sd"], N_SW)

            def gate(j):
                hold(act, G["py"], j * 2)
                nc.scalar.activation(hst[:], Vt[:, bass.ds(j * TW, TW)], ACT.Copy).then_inc(G["hs"], 1)
                for h in range(2):
                    k = j * 2 + h
                    act.wait_ge(G["pw"], k + 1)
                    need(act, G["oT"], k - 1)
                    nc.scalar.activation(ob[:, h], H[2 + h][:], ACT.Identity, bias=col("w2_b")).then_inc(G["oe"], 1)
            pairs(act, gate)

            def feed(j):
                for v in range(2):
                    t = j * 2 + v
                    act.wait_ge(K["nrmT"], t + 1)
                    need(act, K["f1"], (t - 1) * 2)
                    nc.scalar.activation(hT[:, v], T[v][:], ACT.Identity, scale=col("ln2_g"),
                                         bias=col("ln2_b")).then_inc(K["hT"], 1)
                for v in range(2):
                    t = j * 2 + v
                    need(act, K["f2"], t - 1)
                    for c in range(2):
                        act.wait_ge(K["f1"], t * 2 + c + 1)
                        nc.scalar.activation(gel[:, v, c], H[2 * v + c][:], ACT.Gelu,
                                             bias=col("ff1_b", c)).then_inc(K["ge"], 1)
                for v in range(2):
                    t = j * 2 + v
                    act.wait_ge(K["f2"], t + 1)
                    need(act, K["oT"], t - 1)
                    nc.scalar.activation(ob[:, v], Y[v][:], ACT.Identity, bias=col("ff2_b")).then_inc(K["oe"], 1)
            pairs(act, feed)

        def attn_pe():
            pe = nc.tensor
            MM = nc.tensor.matmul

            def mix(j):
                for h in range(2):
                    k = j * 2 + h
                    pe.wait_ge(G["nrm"], k + 1)
                    need(pe, G["hT"], k - 1)
                    transpose_tile(T[h], lambda s: nrm[:, h, s, :], G["nrmT"])
                for h in range(2):
                    k = j * 2 + h
                    pe.wait_ge(G["hT"], k + 1)
                    need(pe, G["x1e"], k - 1)
                    MM(H[2 * h][:], wT[:, W1], hT[:, h], start=True, stop=True).then_inc(G["p1"], 1)
                    need(pe, G["vs"], k - 1)
                    MM(H[2 * h + 1][:], wT[:, V1], hT[:, h], start=True, stop=True).then_inc(G["pv"], 1)
                for h in range(2):
                    k = j * 2 + h
                    pe.wait_ge(G["xc"], k + 1)
                    need(pe, G["ue"], k - 1)
                    MM(Y[h][h * NST:(h + 1) * NST, :], wT[:, BM, 0:NST], xcb[:, h], start=True,
                       stop=True).then_inc(G["pu"], 1)
            pairs(pe, mix)

            pe.wait_ge(G["vs"], NT)
            done = 0
            pe.wait_ge(G["ue"], NT)
            for n, (l, src, _, st, cnt) in enumerate(sweeps()):
                if done:
                    pe.wait_ge(G["sd"], done)
                for b, nb in pieces(cnt):
                    MM(BANKS[done % 4][:, 0:nb * cnt].rearrange("p (b c) -> p b c", c=cnt), pwT[:, l],
                       strided(b, nb, src, st, cnt), start=True, stop=True).then_inc(G["sp"], 1)
                    done += 1
            pe.wait_ge(G["sd"], done)

            def gate(j):
                pe.wait_ge(G["hs"], j + 1)
                for h in range(2):
                    k = j * 2 + h
                    need(pe, G["gm"], k - 1)
                    hs = slice(h * NST, (h + 1) * NST)
                    MM(H[h][:], wT[hs, CM, :], hst[hs, :], start=True, stop=True).then_inc(G["py"], 1)
                for h in range(2):
                    k = j * 2 + h
                    pe.wait_ge(G["gm"], k + 1)
                    need(pe, G["oe"], k - 1)
                    MM(H[2 + h][:], wT[:, W2], cvb[:, h], start=True, stop=True).then_inc(G["pw"], 1)
                for h in range(2):
                    k = j * 2 + h
                    pe.wait_ge(G["oe"], k + 1)
                    need(pe, G["rd"], k - 1)
                    transpose_tile(T[h], lambda s: ob[:, h, s * P:(s + 1) * P], G["oT"])
            pairs(pe, gate)

            pe.wait_ge(G["rd"], NT)

            def feed(j):
                for v in range(2):
                    t = j * 2 + v
                    pe.wait_ge(K["nrm"], t + 1)
                    need(pe, K["xd"], t - 1)
                    transpose_tile(T[v], lambda s: nrm[:, v, s, :], K["nrmT"])
                for v in range(2):
                    t = j * 2 + v
                    pe.wait_ge(K["hT"], t + 1)
                    need(pe, K["ge"], (t - 1) * 2)
                    for c in range(2):
                        MM(H[2 * v + c][:], wT[:, F1 + c], hT[:, v], start=True, stop=True).then_inc(K["f1"], 1)
                for v in range(2):
                    t = j * 2 + v
                    need(pe, K["oe"], t - 1)
                    for c in range(2):
                        pe.wait_ge(K["ge"], t * 2 + c + 1)
                        ins = MM(Y[v][:], wT[:, F2 + c], gel[:, v, c], start=c == 0, stop=c == 1)
                    ins.then_inc(K["f2"], 1)
                for v in range(2):
                    t = j * 2 + v
                    pe.wait_ge(K["oe"], t + 1)
                    transpose_tile(T[v], lambda s: ob[:, v, s * P:(s + 1) * P], K["oT"])
            pairs(pe, feed)

        N_SW = sum(len(pieces(cnt)) for _, _, _, _, cnt in sweeps())

        stage = XA
        W1, V1, W2, F1, F2, BM, CM = 0, 1, 2, 3, 5, 7, 8
        loads = [(stage[:, W1], w1_w), (stage[:, V1], v1_w), (stage[:, W2], w2_w),
                 (stage[:, F1:F1 + 2], ff1_w.rearrange("(c p) d -> p c d", p=P)),
                 (stage[:, F2:F2 + 2], ff2_w.rearrange("p (c d) -> p c d", d=P)),
                 (stage[0:NST, BM], Bm), (stage[:, CM, 0:NST], Cm), (stage[:, CM, NST:P], Cm),
                 (cw[:], conv_w.rearrange("d a k -> d (a k)")), (gw[:], gate_w),
                 (gb[:], gate_b.rearrange("(a e) -> a e", a=1).to_broadcast([P, E]))]
        loads += [(rows[r:r + n, :], ap) for r, n, ap in row_loads]
        N_LD, N_BIG = len(loads), 8
        SQ = 9
        block = ctx.enter_context(nc.Block())

        def w_view(n, k):
            a = (sw1, sw2)[k] if n == 0 else (ew1, ew2)[k][n - 1]
            return a if k == 0 else a.rearrange("(c p) d -> p c d", p=P)

        @block.sync
        def _(sp):
            for dst, src in loads[:N_BIG]:
                sp.dma_start(dst, src).then_inc(s_ld, 16)
            for h in range(2):
                sl = slice(h * HS, (h + 1) * HS)
                sp.dma_start(x_tok[:, sl, :], x_view[:, sl, :]).then_inc(s_x[h], 16)
            for dst, src in loads[N_BIG:]:
                sp.dma_start(dst, src).then_inc(s_ld, 16)
            sp.wait_ge(s_zero, 2)
            for h in range(2):
                sp.dma_start(pw[h * NST:(h + 1) * NST, 0, h * NST:(h + 1) * NST], A).then_inc(s_abd, 16)
            for n in range(NE):
                if n >= 2:
                    sp.wait_ge(s_wlo, n - 1)
                for k in range(2):
                    dst = wstage[:, n % 2, k * WC:(k + 1) * WC]
                    dst = dst if k == 0 else dst.rearrange("p (c d) -> p c d", d=D)
                    sp.dma_start(dst, w_view(n, k)).then_inc(s_wst[n % 2], 16)
                if n in (1, 3):
                    h = n // 2
                    nr = HALF_BLOCKS * SB
                    sp.dma_start(xs_dram[h * nr * P:(h + 1) * nr * P, :].rearrange("(p n) d -> p n d", p=P),
                                 zrow[:, :].unsqueeze(1).to_broadcast([P, nr, P])).then_inc(s_zrow, 16)
            ffn_sp(0)
            ffn_sp(1)
            for h in range(2):
                for q in range(4):
                    sl = slice(h * HS + q * HS // 4, h * HS + (q + 1) * HS // 4)
                    sp.wait_ge(FS[1]["comb"], sl.stop)
                    sp.dma_start(out_view[:, sl, :], x_tok[:, sl, :]).then_inc(s_out, 16)
            sp.wait_ge(s_out, 16 * 8)

        @block.gpsimd
        def _(pool):
            pool.memset(pw[:, 0, :], 0.0).then_inc(s_zero, 1)
            pool.memset(zrow[:], 0.0).then_inc(s_zero, 1)
            pool.memset(ident[:], 0.0).then_inc(s_zero, 1)
            pool.memset(ones[:], 1.0).then_inc(s_zero, 1)
            pool.memset(before[:], 1.0).then_inc(s_zero, 1)
            for e in range(E):
                pool.memset(rank[:, e:e + 1], float(E - e)).then_inc(s_zero, 1)
            pool.iota(starts[:], [[BW, HALF_BLOCKS]], base=0, channel_multiplier=0,
                      allow_small_or_imprecise_dtypes=True).then_inc(s_zero, 1)
            pool.wait_ge(s_zero, 6 + E)
            nc.gpsimd.affine_select(out=ident[:], in_=ident[:], compare_op=ALU.not_equal, fill=1.0, base=0,
                                    pattern=[[-1, P]], channel_multiplier=1).then_inc(s_id, 1)
            nc.gpsimd.affine_select(out=before[:], in_=before[:], compare_op=ALU.is_gt, fill=0.0, base=0,
                                    pattern=[[1, P]], channel_multiplier=-1).then_inc(s_id, 1)
            for n in range(NE):
                pool.wait_ge(s_whi, n + 1)
                w4 = W[:, n].rearrange("p (k q) w -> p k q w", q=2)
                nc.gpsimd.tensor_tensor(w4[:, :, 1], wstage[:, n % 2].rearrange("p (k w) -> p k w", k=2),
                                        w4[:, :, 0].bitcast(F32), ALU.subtract).then_inc(s_wlo, 1)
            ffn_pool(0)
            attn_pool()
            ffn_pool(1)

        @block.scalar
        def _(act):
            for b in range(2):
                act.wait_ge(s_wT, b + 1)
                n = (4 if b == 0 else 3) * P + (0 if b == 0 else NST)
                nc.scalar.activation(wT[:, 4 * b:4 * b + 4].rearrange("p b d -> p (b d)")[:, 0:n], H[b][:, 0:n],
                                     ACT.Copy).then_inc(s_wc, 1)
            act.wait_ge(s_wT, 3)
            nc.scalar.activation(wT[:, CM], H[2][:, 0:P], ACT.Copy).then_inc(s_wc, 1)
            nc.scalar.activation(colv[:], H[2][:, P:P + n_rows], ACT.Copy).then_inc(s_wc, 1)
            nc.scalar.activation(pwT[:, 0], H[2][:, 2 * P:3 * P], ACT.Copy).then_inc(s_wc, 1)
            for l in range(1, SQ):
                act.wait_ge(s_pp, l)
                nc.scalar.activation(pw[:, l % 2], H[3][:, 0:P], ACT.Copy).then_inc(s_pw, 1)
                nc.scalar.activation(pwT[:, l], H[3][:, P:2 * P], ACT.Copy).then_inc(s_pw, 1)
            for n in range(NE):
                act.wait_ge(s_wst[n % 2], 32 * (n // 2 + 1))
                w4 = W[:, n].rearrange("p (k q) w -> p k q w", q=2)
                nc.scalar.activation(w4[:, :, 0], wstage[:, n % 2].rearrange("p (k w) -> p k w", k=2),
                                     ACT.Copy).then_inc(s_whi, 1)
                if n == 1:
                    prepare_act(0, 0)
            prepare_act(0, 1)
            ffn_act(0)
            attn_act()
            prepare_act(1, 0)
            prepare_act(1, 1)
            ffn_act(1)

        @block.vector
        def _(dve):
            ffn_dve(0)
            attn_dve()
            ffn_dve(1)

        @block.tensor
        def _(pe):
            pe.wait_ge(s_id, 2)
            pe.wait_ge(s_ld, 16 * N_LD)
            pe.wait_ge(s_abd, 32)
            TR = nc.tensor.transpose
            for b in range(7):
                ins = TR(H[b // 4][:, b % 4 * P:b % 4 * P + P], stage[:, b], ident[:])
                if b == 3:
                    ins.then_inc(s_wT, 1)
            TR(H[1][:, 3 * P:3 * P + NST], stage[0:NST, BM], ident[0:NST, 0:NST]).then_inc(s_wT, 1)
            TR(H[2][:, 0:P], stage[:, CM], ident[:])
            TR(H[2][:, P:P + n_rows], rows[0:n_rows, :], ident[0:n_rows, 0:n_rows])
            TR(H[2][:, 2 * P:3 * P], pw[:, 0], ident[:]).then_inc(s_wT, 1)
            pe.wait_ge(s_wc, 5)
            for l in range(1, SQ):
                if l > 1:
                    pe.wait_ge(s_pw, 2 * (l - 1))
                nc.tensor.matmul(H[3][:, 0:P], pwT[:, l - 1], pw[:, (l - 1) % 2], start=True, stop=True)
                nc.tensor.matmul(H[3][:, P:2 * P], pw[:, (l - 1) % 2], pwT[:, l - 1], start=True,
                                 stop=True).then_inc(s_pp, 1)
            pe.wait_ge(s_pw, 2 * (SQ - 1))
            ffn_pe(0)
            attn_pe()
            ffn_pe(1)


_INS = ['L0_attn_x', 'L0_attn_w1_w', 'L0_attn_w1_b', 'L0_attn_v1_w', 'L0_attn_v1_b', 'L0_attn_w2_w', 'L0_attn_w2_b',
        'L0_attn_conv_w', 'L0_attn_A', 'L0_attn_Bm', 'L0_attn_Cm', 'L0_attn_ln1_g', 'L0_attn_ln1_b', 'L0_attn_ln2_g',
        'L0_attn_ln2_b', 'L0_attn_ff1_w', 'L0_attn_ff1_b', 'L0_attn_ff2_w', 'L0_attn_ff2_b', 'L0_ffn_gate_w',
        'L0_ffn_gate_b', 'L0_ffn_w1', 'L0_ffn_b1', 'L0_ffn_w2', 'L0_ffn_b2', 'L0_ffn_ws1', 'L0_ffn_bs1', 'L0_ffn_ws2',
        'L0_ffn_bs2']
_OUTS = [((8, 512, 128), 'float32')]


def kernel(**inputs):
    import numpy as _np
    import concourse.bacc as _bacc
    from concourse import mybir as _mybir
    from concourse.bass_utils import run_bass_kernel_spmd as _run

    nc = _bacc.Bacc("TRN2", target_bir_lowering=False, num_devices=1)
    arrays, args = {}, []
    for name in _INS:
        a = _np.ascontiguousarray(inputs[name])
        arrays[f"in_{name}_dram"] = a
        args.append(nc.dram_tensor(f"in_{name}_dram", a.shape, _mybir.dt.from_np(a.dtype), kind="ExternalInput").ap())
    for i, (shape, dtype) in enumerate(_OUTS):
        dt = _mybir.dt.from_np(_np.dtype(dtype))
        args.append(nc.dram_tensor(f"out_{i}_dram", shape, dt, kind="ExternalOutput").ap())
    macaron_kernel(nc, *args)
    r = _run(nc, [arrays], core_ids=[0])
    got = tuple(r.results[0][f"out_{i}_dram"] for i in range(len(_OUTS)))
    return got[0]
```

```python
from contextlib import ExitStack

import numpy as np
import concourse.bass as bass
from concourse import mybir

F32 = mybir.dt.float32
F32R = mybir.dt.float32r
I32 = mybir.dt.int32
ALU = mybir.AluOpType
ACT = mybir.ActivationFunctionType
AX = mybir.AxisListType

P = 128
TW = 512
SUB = TW // P
BW = 256
SB = BW // P
EPS = 1e-5
NEG = -3.0e38
CH = 16
RSQRT_SEED = float(0x5F3759DF)


def macaron_kernel(nc, x, w1_w, w1_b, v1_w, v1_b, w2_w, w2_b, conv_w, A, Bm, Cm, ln1_g, ln1_b, ln2_g, ln2_b,
                   ff1_w, ff1_b, ff2_w, ff2_b, gate_w, gate_b, ew1, eb1, ew2, eb2, sw1, sb1, sw2, sb2, out):
    NB, TS, D = x.shape
    E, _, HID = ew1.shape
    HC = HID // P
    WC = HC * P
    NT = NB * TS // TW
    NS = NT * SUB
    HS = NS // 2
    NST = A.shape[0]
    HB = NT // 2
    HALF_BLOCKS = (2 * HS * P - E) // BW + E
    NBLK = 2 * HALF_BLOCKS
    SHBLK = NS // SB
    assert D == P and TS == TW and NST * 2 == P and HS * E == P

    x_view = x.rearrange("b (s p) d -> p (b s) d", p=P)
    out_view = out.rearrange("b (s p) d -> p (b s) d", p=P)

    cols, n_rows, row_loads = {}, 0, []
    for name, ap, n in (("b1", sb1.rearrange("(c p) -> c p", p=P), HC), ("eb1", eb1.rearrange("e (c p) -> (e c) p", p=P), E * HC),
                        ("b2", sb2, 1), ("eb2", eb2, E), ("w1_b", w1_b, 1),
                        ("v1_b", v1_b, 1), ("w2_b", w2_b, 1), ("ln1_g", ln1_g, 1), ("ln1_b", ln1_b, 1),
                        ("ln2_g", ln2_g, 1), ("ln2_b", ln2_b, 1), ("ff1_b", ff1_b.rearrange("(c p) -> c p", p=P), 2),
                        ("ff2_b", ff2_b, 1)):
        if len(ap.shape) == 1:
            ap = ap.rearrange("(a p) -> a p", a=1)
        cols[name] = n_rows
        row_loads.append((n_rows, n, ap))
        n_rows += n

    xs_dram = nc.dram_tensor("sorted_x_dram", (NBLK * BW, D), F32).ap()
    ys_dram = nc.dram_tensor("sorted_y_dram", (NBLK * BW, D), F32).ap()

    with ExitStack() as ctx:
        def sb(name, shape, dt=F32, scope=ctx):
            return scope.enter_context(nc.sbuf_tensor(name, shape, dt))

        def sem(name):
            return ctx.enter_context(nc.semaphore(name))

        x_tok = sb("x_tok", [P, NS, D])
        W = sb("W", [P, E + 1, 4, WC], F32R)
        GB = sb("GB", [P, 2, HS, D])
        res_tok = GB[:, :, :, :].rearrange("p a s d -> p (a s) d")
        wstage = GB[:, 1].rearrange("p (u w) d -> p u (w d)", u=2)
        XA = sb("XA", [P, HS, D])
        XN = lambda i: XA[:, i, :] if i < HS else GB[:, 0, i - HS, :]
        stats = sb("stats", [P, NS, 6])
        mean = sb("mean", [P, NS])
        lnt = sb("lnt", [P, 5, NS])
        ve = sb("ve", [P, NS])
        rstd = sb("rstd", [P, NS])
        ident = sb("ident", [P, P])
        before = sb("before", [P, P])
        ones = sb("ones", [P, P])
        rows = sb("rows", [P, P])
        colv = sb("colv", [P, n_rows])
        cw = sb("cw", [P, 3])
        zrow = sb("zrow", [P, D])
        gb = sb("gb", [P, E])
        gw = sb("gw", [P, E])
        rank = sb("rank", [P, E])
        starts = sb("starts", [P, HALF_BLOCKS])
        lt, ta, tb, sel1, sel2 = (sb(f"route_{k}", [P, NS, E]) for k in ("logit", "a", "b", "sel1", "sel2"))
        m1, m2, k1, k2, dd, ex, sm = (sb(f"route_{k}", [P, NS]) for k in ("m1", "m2", "k1", "k2", "d", "ex", "sum"))
        wab = sb("wab", [P, 2, NS])
        posf = sb("posf", [P, 2, NS])
        posI = sb("posI", [P, 2, NS], I32)
        cntI = sb("cntI", [P, 2, 2, E], I32)
        ends = sb("ends", [P, 3, 2, E])
        cmp_ = sb("cmp", [1, 2, HALF_BLOCKS, E])
        eidf = sb("eidf", [1, NBLK])
        eid = sb("eid", [1, NBLK], I32)
        wT = sb("wT", [P, 9, P])
        pwT = sb("pwT", [P, 9, P])
        pw = sb("pw", [P, 2, P])
        with ExitStack() as phase:
            w1r = sb("w1r", [P, 2, 2, WC], F32R, phase)
            w2r = sb("w2r", [P, 2, 2, WC], F32R, phase)
            hf = sb("hf", [P, 2, HC, BW], F32, phase)
            hhi = sb("hhi", [P, 2, HC, BW], F32R, phase)
            hlo = sb("hlo", [P, 2, HC, BW], F32R, phase)
            xin = sb("xin", [P, 2, SB, D], F32, phase)
            xbhi = sb("xbhi", [P, 2, BW], F32R, phase)
            xblo = sb("xblo", [P, 2, BW], F32R, phase)
            yT = sb("yT", [P, 2, BW], F32, phase)
            yo = sb("yo", [P, 2, BW], F32, phase)
            xfT = sb("xfT", [P, NS * P], F32, phase)
            GBB = xfT[:, :].rearrange("p (k s d) -> p k s d", k=2, d=D)
        with ExitStack() as phase:
            v_all = sb("v_all", [P, NT * TW], F32, phase)
            Vt = sb("Vt", [P, HB * TW], F32, phase)
            nrm = sb("nrm", [P, 2, SUB, P], F32, phase)
            hT = sb("hT", [P, 2, TW], F32, phase)
            cvb = sb("cvb", [P, 2, TW], F32, phase)
            xcb = sb("xcb", [P, 2, TW], F32, phase)
            x1p = sb("x1p", [P, 2, TW + 2], F32, phase)
            used = NT * TW + HB * TW + 2 * SUB * P + 6 * TW + 2 * (TW + 2)
            sb("below_xfT", [P, 2 * 4 * WC + 3 * 2 * HC * BW + 5 * 2 * BW - used], F32, phase)
            gel = sb("gel", [P, 2, 2, TW], F32, phase)
            hst = sb("hst", [P, TW], F32, phase)
            ob = sb("ob", [P, 2, TW], F32, phase)

        H = [ctx.enter_context(nc.psum_tensor(f"H{c}", [P, TW], F32)) for c in range(HC)]
        Y = [ctx.enter_context(nc.psum_tensor(f"Y{c}", [P, TW], F32)) for c in range(2)]
        T = [ctx.enter_context(nc.psum_tensor(f"T{c}", [P, TW], F32)) for c in range(2)]
        TX, TY = T

        def col(name, k=0):
            return colv[:, cols[name] + k:cols[name] + k + 1]

        s_x = [sem(f"x{h}_loaded") for h in range(2)]
        s_wst = [sem(f"expert_weights{u}_loaded") for u in range(2)]
        s_whi = sem("expert_weights_hi")
        s_wlo = sem("expert_weights_lo")
        s_zrow = sem("rows_zeroed")
        s_bord = sem("borders_zeroed")
        s_ld = sem("constants_loaded")
        s_zero = sem("constants_zeroed")
        s_abd = sem("A_blocks_loaded")
        s_id = sem("ident_ready")
        s_wT = sem("weights_transposed")
        s_wc = sem("weights_ready")
        s_pp = sem("power_squared")
        s_pw = sem("power_ready")
        s_out = sem("out_stored")
        s_own = sem("held")
        s_chain = sem("vector_chain")
        chain = [0]

        def link(ins):
            chain[0] += 1
            ins.then_inc(s_chain, 1)
            nc.vector.wait_ge(s_chain, chain[0])

        def count(ins):
            chain[0] += 1
            ins.then_inc(s_chain, 1)

        def need(eng, s, v):
            if not isinstance(v, int) or v > 0:
                eng.wait_ge(s, v)

        def hold(eng, s, v):
            if not isinstance(v, int) or v > 0:
                eng.wait_ge(s, v)
                eng.sem_inc(s_own, 1)

        def pairs(eng, body):
            body(0)
            with eng.Fori(1, NT // 2) as j:
                body(j)

        def pipeline(eng, n, step):
            for b in (-1, 0, 1):
                step(b, b % 2)
            inner = (n - 3) // 2
            with eng.Fori(1, 1 + inner) as j:
                for u in range(2):
                    step(j * 2 + u, u)
            for b in range(2 + 2 * inner, n + 2):
                step(b, b % 2)

        def exists(b, n):
            return not isinstance(b, int) or 0 <= b < n

        FN = ["nrm", "nrmT", "xfT", "gates", "m", "pre", "d", "ex", "pos", "sc0", "sc1",
              "ga0", "ga1", "ga2", "ga3", "gb0", "gb1", "gb2", "gb3", "x2", "comb"]
        FS = [{n: sem(f"ffn{f}_{n}") for n in FN} for f in range(2)]
        BN = ["TX", "xhi", "xlo", "w1", "w2", "up", "gelu", "hhi", "split", "y", "yT", "TY", "yo", "in0", "in1",
              "st0", "st1", "wl0", "wl1"]
        BS = [[{n: sem(f"ffn{f}_{k}_{n}") for n in BN if k == "routed" or n not in ("w1", "w2", "in0", "in1", "st0", "st1", "wl0", "wl1")}
               for k in ("shared", "routed")] for f in range(2)]
        GN = ["res", "nrm", "nrmT", "hT", "p1", "pv", "x1e", "vs", "c1", "c2", "cv", "xc", "pu", "ue", "sp", "sd", "hs", "py",
              "gm", "pw", "oe", "oT", "rd"]
        G = {n: sem(f"attn_{n}") for n in GN}
        KN = ["nrm", "nrmT", "hT", "f1", "ge", "f2", "oe", "oT", "xr", "xd"]
        K = {n: sem(f"ff_{n}") for n in KN}

        def slot(t):
            return bass.ds(t * SUB, SUB)

        def tile(t):
            return bass.ds(t * TW, TW)

        def ln(src, lo=0, hi=None):
            hi = NS if hi is None else hi
            TT, TS, STT = nc.vector.tensor_tensor, nc.vector.tensor_scalar, nc.vector.scalar_tensor_tensor
            r = slice(lo, hi)
            for i in range(lo, hi):
                nc.vector.bn_stats(stats[:, i, :], src(i)).then_inc(s_chain, 1)
            chain[0] += hi - lo
            nc.vector.wait_ge(s_chain, chain[0])
            count(TT(lnt[:, 0, r], stats[:, r, 1], stats[:, r, 4], ALU.add))
            count(TT(lnt[:, 1, r], stats[:, r, 1], stats[:, r, 4], ALU.subtract))
            link(TT(lnt[:, 2, r], stats[:, r, 2], stats[:, r, 5], ALU.add))
            count(TS(mean[:, r], lnt[:, 0, r], 0.5, None, ALU.mult))
            count(TT(lnt[:, 3, r], lnt[:, 1, r], lnt[:, 1, r], ALU.mult))
            link(TS(lnt[:, 4, r], lnt[:, 2, r], 1.0 / D, EPS, ALU.mult, ALU.add))
            link(STT(ve[:, r], lnt[:, 3, r], 0.25, lnt[:, 4, r], ALU.mult, ALU.add))
            y0, sq, vy = lnt[:, 0, r], lnt[:, 1, r], lnt[:, 2, r]
            link(TS(y0.bitcast(I32), ve[:, r].bitcast(I32), -0.5, RSQRT_SEED, ALU.mult, ALU.add))
            steps = 4
            for i in range(steps):
                link(TT(sq, y0, y0, ALU.mult))
                link(STT(vy, sq, -0.5, ve[:, r], ALU.mult, ALU.mult))
                link(STT(rstd[:, r] if i == steps - 1 else y0, vy, 1.5, y0, ALU.add, ALU.mult))

        def normalise(dst, src, t, done):
            for s in range(SUB):
                i = t * SUB + s
                ins = nc.vector.tensor_scalar(dst[:, s, :], src[:, i, :], mean[:, bass.ds(i, 1)],
                                              rstd[:, bass.ds(i, 1)], ALU.subtract, ALU.mult)
            ins.then_inc(done, 1)

        def transpose_tile(bank, src, done):
            for s in range(SUB):
                ins = nc.tensor.transpose(bank[:, s * P:(s + 1) * P], src(s), ident[:])
            ins.then_inc(done, 1)

        NE = E + 1

        def scattered(sp, f, h):
            sp.wait_ge(FS[f][f"sc{h}"], 16 * 2 * HS)

        def ffn_sp(f):
            sp, S = nc.sync, BS[f][1]

            def load(b, u):
                rows_in(b, u)
                if not isinstance(b, int) or b > 0:
                    w2_lo(b - 1, 1 - u)

            def rows_in(b, u):
                need(sp, S["TX"], b - 1)
                sp.dma_start(xin[:, u], xs_dram[bass.ds(b * BW, BW), :].rearrange("(s p) d -> p s d", p=P)
                             ).then_inc(S[f"in{u}"], 16)

            def w2_lo(b, u):
                e = sp.value_load(eid[0:1, bass.ds(b, 1)], min_val=1, max_val=E)
                need(sp, S["y"], b - 1)
                sp.dma_start(w2r[:, u, 1].bitcast(F32), W[:, e, 3].bitcast(F32)).then_inc(S[f"wl{u}"], 16)

            def span(lo, hi):
                while lo < hi and (lo < 2 or lo % 2):
                    load(lo, lo % 2)
                    lo += 1
                with sp.Fori(lo // 2, hi // 2) as j:
                    for u in range(2):
                        load(j * 2 + u, u)
                if hi % 2:
                    load(hi - 1, 0)

            sp.wait_ge(FS[f]["pos"], 2)
            scattered(sp, f, 0)
            span(0, HALF_BLOCKS)
            scattered(sp, f, 1)
            span(HALF_BLOCKS, NBLK)
            w2_lo(NBLK - 1, (NBLK - 1) % 2)

        def ffn_pool(f):
            pool, S, B = nc.gpsimd, FS[f], BS[f][1]

            def rows_of(h, k, s):
                return bass.IndirectOffsetOnAxis(posI[:, k, h * HS + s:h * HS + s + 1], 0)

            def scatter(h):
                pool.wait_ge(s_zrow, 16 * 2)
                if f:
                    pool.wait_ge(BS[0][1]["in0"], 16 * (NBLK // 2))
                    pool.wait_ge(BS[0][1]["in1"], 16 * (NBLK // 2))
                pool.wait_ge(S["nrm"], NS)
                pool.wait_ge(S["pos"], 1)
                for s in range(HS):
                    for k in range(2):
                        pool.indirect_dma_start(xs_dram[:, :], rows_of(h, k, s), XN(h * HS + s),
                                                None).then_inc(S[f"sc{h}"], 16)

            def gather(h):
                ends_ = (h + 1) * HALF_BLOCKS
                pool.wait_ge(B["st0"], 16 * ((ends_ + 1) // 2))
                pool.wait_ge(B["st1"], 16 * (ends_ // 2))
                for q in range(4):
                    for s in range(q * HS // 4, (q + 1) * HS // 4):
                        for k in range(2):
                            pool.indirect_dma_start((GB, GBB)[h][:, k, s, :], None, ys_dram[0:ends_ * BW, :],
                                                    rows_of(h, k, s)).then_inc(S[f"g{'ab'[h]}{q}"], 16)

            scatter(0)
            scatter(1)
            pool.wait_ge(S["sc1"], 16 * 2 * HS)
            gather(0)
            gather(1)

        def routed_act(f, S, shared, n):
            act = nc.scalar

            def step(b, u):
                v = 1 - u
                if exists(b + 1, n):
                    need(act, S["up"], b * HC if isinstance(b, int) else b * HC)
                    if shared:
                        hold(act, s_whi, 1)
                        nc.scalar.activation(xbhi[:, v], xfT[:, bass.ds((b + 1) * BW, BW)],
                                             ACT.Copy).then_inc(S["xhi"], 1)
                    else:
                        act.wait_ge(S["TX"], b + 2)
                        nc.scalar.activation(xbhi[:, v], TX[:, 0:BW], ACT.Copy).then_inc(S["xhi"], 1)
                if exists(b, n):
                    need(act, S["split"], b - 1)
                    e = None if shared else act.value_load(eid[0:1, bass.ds(b, 1)], min_val=1, max_val=E)
                    for c in range(HC):
                        hold(act, S["up"], b * HC + c + 1)
                        bias = col("b1", c) if shared else colv[:, bass.ds(e * HC + (cols["b1"] + c), 1)]
                        nc.scalar.activation(hf[:, u, c], H[c][:, 0:BW], ACT.Gelu, bias=bias).then_inc(S["gelu"], 1)
                if exists(b - 2, n) and not shared:
                    act.wait_ge(S["TY"], b - 1)
                    if not (isinstance(b, int) and b - 4 < 0):
                        act.wait_ge(S[f"st{u}"], st_count(b, u))
                    nc.scalar.activation(yo[:, u], TY[:, 0:BW], ACT.Copy).then_inc(S["yo"], 1)
                if exists(b - 1, n):
                    need(act, S["TY"], b - 2)
                    hold(act, S["y"], b)
                    if shared:
                        bias = col("b2")
                    else:
                        e2 = act.value_load(eid[0:1, bass.ds(b - 1, 1)], min_val=1, max_val=E)
                        bias = colv[:, bass.ds(e2 + cols["b2"], 1)]
                    nc.scalar.activation(yT[:, v], Y[v][:, 0:BW], ACT.Identity, bias=bias).then_inc(S["yT"], 1)
                if exists(b, n) and not shared:
                    hold(act, S["y"], b - 1)
                    nc.scalar.activation(w2r[:, u, 0], W[:, e, 2].bitcast(F32), ACT.Copy).then_inc(S["w2"], 1)
                if exists(b - 2, n) and not shared:
                    act.wait_ge(S["yo"], b - 1)
                    act.dma_start(ys_dram[bass.ds((b - 2) * BW, BW), :].rearrange("(s p) d -> p s d", p=P),
                                  yo[:, u].rearrange("p (s d) -> p s d", d=D)).then_inc(S[f"st{u}"], 16)
            pipeline(act, n, step)

        def st_count(b, u):
            return 16 * ((b - 4) // 2 + 1) if isinstance(b, int) else (b - (2 + u)) * 8

        def routed_dve(f, S, shared, n):
            dve = nc.vector
            TT = nc.vector.tensor_tensor

            def step(b, u):
                v = 1 - u
                if exists(b + 1, n):
                    if not shared:
                        e = dve.value_load(eid[0:1, bass.ds(b + 1, 1)], min_val=1, max_val=E)
                        need(dve, S["up"], b * HC)
                        nc.vector.tensor_copy(w1r[:, v].rearrange("p a w -> p (a w)"),
                                              W[:, e, 0:2].rearrange("p a w -> p (a w)").bitcast(F32)
                                              ).then_inc(S["w1"], 1)
                    else:
                        need(dve, S["up"], b * HC)
                    dve.wait_ge(S["xhi"], b + 2)
                    x32 = xfT[:, bass.ds((b + 1) * BW, BW)] if shared else TX[:, 0:BW]
                    TT(xblo[:, v], x32, xbhi[:, v].bitcast(F32), ALU.subtract).then_inc(S["xlo"], 1)
                if exists(b, n):
                    need(dve, S["y"], b - 1)
                    dve.wait_ge(S["gelu"], b * HC + HC)
                    nc.vector.tensor_copy(hhi[:, u], hf[:, u]).then_inc(S["hhi"], 1)
                if exists(b - 2, n) and shared:
                    dve.wait_ge(S["TY"], b - 1)
                    xs = x_tok[:, bass.ds((b - 2) * SB, SB), :]
                    nc.vector.scalar_tensor_tensor(xs, TY[:, 0:BW].rearrange("p (s d) -> p s d", d=D), 0.5, xs,
                                                   ALU.mult, ALU.add).then_inc(S["yo"], 1)
                if exists(b, n):
                    dve.wait_ge(S["hhi"], b + 1)
                    TT(hlo[:, u], hf[:, u], hhi[:, u].bitcast(F32), ALU.subtract).then_inc(S["split"], 1)
            pipeline(dve, n, step)

        def routed_pe(f, S, shared, n):
            pe = nc.tensor
            MM = nc.tensor.matmul

            def step(b, u):
                v = 1 - u
                if exists(b + 1, n) and not shared:
                    pe.wait_ge(S[f"in{v}"], 16 * ((b + 1) // 2 + 1) if isinstance(b, int) else (b + (3 - v)) * 8)
                    need(pe, S["xlo"], b + 1)
                    for s in range(SB):
                        ins = nc.tensor.transpose(TX[:, s * P:(s + 1) * P], xin[:, v, s, :], ident[:])
                    ins.then_inc(S["TX"], 1)
                if exists(b, n):
                    whi, wlo = (W[:, 0, 0], W[:, 0, 1]) if shared else (w1r[:, u, 0], w1r[:, u, 1])
                    pe.wait_ge(S["xlo"], b + 1)
                    if not shared:
                        pe.wait_ge(S["w1"], b + 1)
                    for c in range(HC):
                        need(pe, S["gelu"], (b - 1) * HC + c + 1)
                        ws = slice(c * P, (c + 1) * P)
                        MM(H[c][:, 0:BW], whi[:, ws], xbhi[:, u], start=True, stop=False)
                        MM(H[c][:, 0:BW], whi[:, ws], xblo[:, u], start=False, stop=False)
                        MM(H[c][:, 0:BW], wlo[:, ws], xbhi[:, u], start=False, stop=True).then_inc(S["up"], 1)
                if exists(b - 2, n):
                    pe.wait_ge(S["yT"], b - 1)
                    need(pe, S["yo"], b - 2)
                    for s in range(SB):
                        ins = nc.tensor.transpose(TY[:, s * P:(s + 1) * P], yT[:, u, s * P:(s + 1) * P], ident[:])
                    ins.then_inc(S["TY"], 1)
                if exists(b - 1, n):
                    whi, wlo = (W[:, 0, 2], W[:, 0, 3]) if shared else (w2r[:, v, 0], w2r[:, v, 1])
                    pe.wait_ge(S["split"], b)
                    if not shared:
                        pe.wait_ge(S["w2"], b)
                        pe.wait_ge(S[f"wl{v}"], 16 * ((b - 1) // 2 + 1) if isinstance(b, int) else (b + (1 - v)) * 8)
                    need(pe, S["yT"], b - 2)
                    for c in range(HC):
                        ws = slice(c * P, (c + 1) * P)
                        MM(Y[v][:, 0:BW], whi[:, ws], hhi[:, v, c], start=c == 0, stop=False)
                        MM(Y[v][:, 0:BW], whi[:, ws], hlo[:, v, c], start=False, stop=False)
                        ins = MM(Y[v][:, 0:BW], wlo[:, ws], hhi[:, v, c], start=False, stop=c == HC - 1)
                    ins.then_inc(S["y"], 1)
            pipeline(pe, n, step)

        def prepare_dve(f):
            dve, S = nc.vector, FS[f]
            if f == 0:
                dve.wait_ge(s_x[0], 16)
                dve.wait_ge(s_x[1], 16)
            else:
                dve.wait_ge(K["xd"], NT)
            ln(lambda i: x_tok[:, i, :])
            if f == 0:
                dve.wait_ge(s_wT, 3)
            for i in range(NS):
                nc.vector.tensor_scalar(XN(i), x_tok[:, i, :], mean[:, i:i + 1], rstd[:, i:i + 1], ALU.subtract,
                                        ALU.mult).then_inc(S["nrm"], 1)

        def prepare_pe(f):
            pe, S = nc.tensor, FS[f]
            for t in range(NT):
                pe.wait_ge(S["nrm"], (t + 1) * SUB)
                need(pe, S["xfT"], t - HC + 1)
                transpose_tile(H[t % HC], lambda s: XN(t * SUB + s), S["nrmT"])
            for t in range(NT):
                pe.wait_ge(S["xfT"], t + 1)
                for s in range(SUB):
                    i = t * SUB + s
                    c = (i % HS) * E
                    ins = nc.tensor.matmul(Y[i // HS][:, c:c + E], xfT[:, i * P:(i + 1) * P], gw[:], start=True,
                                           stop=True)
            ins.then_inc(S["gates"], 1)
            pe.wait_ge(S["m"], 1)
            ms = ta[:, :, :].rearrange("p s e -> p (s e)")
            nc.tensor.matmul(TX[:, 0:2 * P], before[:], ms, start=True, stop=True)
            nc.tensor.matmul(TX[:, 2 * P:4 * P], ones[:], ms, start=True, stop=True).then_inc(S["pre"], 1)

        def prepare_act(f):
            act, S = nc.scalar, FS[f]
            for t in range(NT):
                act.wait_ge(S["nrmT"], t + 1)
                nc.scalar.activation(xfT[:, t * TW:(t + 1) * TW], H[t % HC][:], ACT.Copy).then_inc(S["xfT"], 1)

        def softmax_act(f):
            nc.scalar.wait_ge(FS[f]["d"], 1)
            nc.scalar.activation(ex[:], dd[:], ACT.Exp).then_inc(FS[f]["ex"], 1)

        def route_dve(f):
            dve, S = nc.vector, FS[f]
            ex3 = lambda a: a.unsqueeze(2).to_broadcast([P, NS, E])
            tok3 = lambda a: a.unsqueeze(1).to_broadcast([P, NS, E])
            TT, TR, TS = nc.vector.tensor_tensor, nc.vector.tensor_reduce, nc.vector.tensor_scalar
            STT = nc.vector.scalar_tensor_tensor
            dve.wait_ge(S["gates"], 1)
            dve.wait_ge(s_ld, 16 * N_LD)
            for h in range(2):
                ins = TT(lt[:, h * HS:(h + 1) * HS], Y[h][:, 0:P].rearrange("p (s e) -> p s e", e=E),
                         tok3(gb[:])[:, 0:HS], ALU.add)
                (link if h else count)(ins)

            def pick(m, key, sel):
                link(TR(m[:], lt[:], AX.X, ALU.max))
                link(TT(ta[:], lt[:], ex3(m[:]), ALU.is_equal))
                link(TT(tb[:], ta[:], tok3(rank[:]), ALU.mult))
                link(TR(key[:], tb[:], AX.X, ALU.max))
                link(TT(sel[:], tok3(rank[:]), ex3(key[:]), ALU.is_equal))
            pick(m1, k1, sel1)
            link(TS(ta[:], sel1[:], -1.0, 1.0, ALU.mult, ALU.add))
            link(TT(tb[:], lt[:], ta[:], ALU.mult))
            link(STT(lt[:], sel1[:], NEG, tb[:], ALU.mult, ALU.add))
            pick(m2, k2, sel2)
            TT(dd[:], m2[:], m1[:], ALU.subtract).then_inc(S["d"], 1)
            TT(ta[:], sel1[:], sel2[:], ALU.add).then_inc(S["m"], 1)
            dve.wait_ge(S["ex"], 1)
            link(TS(sm[:], ex[:], 1.0, None, ALU.add))
            link(nc.vector.reciprocal(m1[:], sm[:]))
            link(TT(m2[:], ex[:], m1[:], ALU.mult))
            TS(wab[:, 0], m1[:], 0.5, None, ALU.mult).then_inc(S["x2"], 1)
            TS(wab[:, 1], m2[:], 0.5, None, ALU.mult).then_inc(S["x2"], 1)
            dve.wait_ge(S["pre"], 1)
            pre = TX[:, 0:2 * P].rearrange("p (s e) -> p s e", e=E)
            tot = TX[:, 2 * P:4 * P].rearrange("p (s e) -> p s e", e=E)
            by_half = lambda a: a.rearrange("p (h s) e -> p h s e", h=2)
            for h in range(2):
                r = slice(h * HS, (h + 1) * HS)
                for e in range(E):
                    ins = nc.vector.tensor_tensor_scan(tb[:, r, e], ones[:, 0:HS], tot[:, r, e], 0.0, ALU.mult,
                                                       ALU.add)
            link(ins)
            link(TS(cntI[:, 0], by_half(tb[:, :, :])[:, :, HS - 1, :], float(BW - 1), None, ALU.add))
            link(TS(cntI[:, 1], cntI[:, 0], BW.bit_length() - 1, BW.bit_length() - 1, ALU.logical_shift_right,
                    ALU.logical_shift_left))
            link(nc.vector.tensor_copy(ends[:, 0], cntI[:, 1]))
            for h in range(2):
                ins = nc.vector.tensor_tensor_scan(ends[:, 1, h], ones[:, 0:E], ends[:, 0, h], 0.0, ALU.mult, ALU.add)
                (link if h else count)(ins)
            count(TT(ends[:, 2, 0], ends[:, 1, 0], ends[:, 0, 0], ALU.subtract))
            count(STT(ends[:, 2, 1], ends[:, 1, 1], float(HALF_BLOCKS * BW), ends[:, 0, 1], ALU.add, ALU.subtract))
            link(TT(ta[:], tb[:], tot, ALU.subtract))
            link(TT(tb[:], ta[:], pre, ALU.add))
            link(TT(by_half(ta[:, :, :]), by_half(tb[:, :, :]), ends[:, 2].unsqueeze(2).to_broadcast([P, 2, HS, E]),
                    ALU.add))
            count(TT(tb[:], ta[:], sel1[:], ALU.mult))
            link(TT(lt[:], ta[:], sel2[:], ALU.mult))
            count(TR(posf[:, 0], tb[:], AX.X, ALU.add))
            link(TR(posf[:, 1], lt[:], AX.X, ALU.add))
            nc.vector.tensor_copy(posI[:], posf[:]).then_inc(S["pos"], 1)
            NBH = [1, 2, HALF_BLOCKS, E]
            link(TT(cmp_[:], starts[0:1, :].unsqueeze(1).unsqueeze(3).to_broadcast(NBH),
                    ends[0:1, 1].unsqueeze(2).to_broadcast(NBH), ALU.is_ge))
            link(TR(eidf[:].rearrange("a (h b) -> a h b", h=2), cmp_[:], AX.X, ALU.add))
            TS(eid[:], eidf[:], float(E - 1), 1.0, ALU.min, ALU.add).then_inc(S["pos"], 1)

        def combine(f, h):
            dve, S = nc.vector, FS[f]
            for q in range(4):
                dve.wait_ge(S[f"g{'ab'[h]}{q}"], 16 * 2 * HS // 4)
                for k in range(2):
                    for s in range(q * HS // 4, (q + 1) * HS // 4):
                        xs = x_tok[:, h * HS + s, :]
                        if k:
                            dve.wait_ge(S["x2"], 2 + h * HS + s + 1)
                        nc.vector.scalar_tensor_tensor(xs, (GB, GBB)[h][:, k, s, :], wab[:, k, h * HS + s:h * HS + s + 1], xs, ALU.mult,
                                                       ALU.add).then_inc(S["comb" if k else "x2"], 1)

        def ffn_dve(f):
            prepare_dve(f)
            route_dve(f)
            routed_dve(f, BS[f][0], True, SHBLK)
            nc.vector.wait_ge(s_wlo, NE)
            routed_dve(f, BS[f][1], False, NBLK)
            nc.vector.wait_ge(BS[f][0]["yo"], SHBLK)

        def ffn_act(f):
            routed_act(f, BS[f][0], True, SHBLK)
            nc.scalar.wait_ge(s_wlo, NE)
            nc.scalar.wait_ge(FS[f]["pos"], 2)
            routed_act(f, BS[f][1], False, NBLK)

        def ffn_pe(f):
            prepare_pe(f)
            nc.tensor.wait_ge(s_wlo, 1)
            routed_pe(f, BS[f][0], True, SHBLK)
            routed_pe(f, BS[f][1], False, NBLK)

        V = Vt[:, :].rearrange("p (b t) -> p b t", t=TW)
        BANKS = H

        def at(j, h):
            return j * 2 + h

        def sweeps():
            L = CH.bit_length() - 1
            out_ = []
            for l in range(L):
                s = 1 << l
                out_.append((l, s - 1, 2 * s - 1, 2 * s, TW // (2 * s)))
            k = 1
            while k < TW // CH:
                out_.append((L + k.bit_length() - 1, CH - 1, CH - 1 + CH * k, CH, TW // CH - k))
                k *= 2
            for l in reversed(range(L)):
                s = 1 << l
                out_.append((l, 2 * s - 1, 3 * s - 1, 2 * s, TW // (2 * s) - 1))
            return out_

        def pieces(cnt):
            nb = max(1, min(HB, TW // cnt))
            return [(b, min(nb, HB - b)) for b in range(0, HB, nb)]

        def strided(b, nb, first, stride, cnt):
            return V[:, b:b + nb, first:first + stride * (cnt - 1) + 1:stride]

        def attn_dve():
            dve = nc.vector
            TT, STT = nc.vector.tensor_tensor, nc.vector.scalar_tensor_tensor
            dve.wait_ge(s_ld, 16 * N_LD)

            def norms(h):
                sl = range(h * HS, (h + 1) * HS)
                combine(0, h)
                dve.wait_ge(FS[0]["comb"], sl.stop)
                ln(lambda i: x_tok[:, i, :], sl.start, sl.stop)
                for i in sl:
                    nc.vector.tensor_scalar(res_tok[:, i, :], x_tok[:, i, :], mean[:, i:i + 1], rstd[:, i:i + 1],
                                            ALU.subtract, ALU.mult).then_inc(G["res"], 1)
                dve.wait_ge(G["res"], sl.stop)
                ln(lambda i: res_tok[:, i, :], sl.start, sl.stop)

            def mix(j):
                for h in range(2):
                    need(dve, G["nrmT"], j * 2 + h - 1)
                    normalise(nrm[:, h], res_tok, at(j, h), G["nrm"])
                for h in range(2):
                    k = j * 2 + h
                    dve.wait_ge(G["x1e"], k + 1)
                    need(dve, G["xc"], k - 1)
                    nc.vector.tensor_scalar(cvb[:, h], x1p[:, h, 0:TW], cw[:, 0:1], None, ALU.mult).then_inc(G["c1"], 1)
                for i in (1, 2):
                    for h in range(2):
                        k = j * 2 + h
                        dve.wait_ge(G["c1" if i == 1 else "c2"], k + 1)
                        STT(cvb[:, h], x1p[:, h, i:i + TW], cw[:, i:i + 1], cvb[:, h], ALU.mult,
                            ALU.add).then_inc(G["c2" if i == 1 else "cv"], 1)
                for h in range(2):
                    dve.wait_ge(G["pu"], j * 2 + h + 1)
                    hs = slice(h * NST, (h + 1) * NST)
                    nc.vector.tensor_copy(Vt[hs, bass.ds(j * TW, TW)], Y[h][hs, :]).then_inc(G["ue"], 1)
            norms(0)
            for u in range(2):
                dve.wait_ge(BS[0][1][f"st{u}"], 16 * NBLK // 2)
            mix(0)
            mix(1)
            norms(1)
            with dve.Fori(2, NT // 2) as j:
                mix(j)

            done = 0
            dve.wait_ge(G["ue"], NT)
            for n, (_, _, dst, st, cnt) in enumerate(sweeps()):
                for b, nb in pieces(cnt):
                    dve.wait_ge(G["sp"], done + 1)
                    v = strided(b, nb, dst, st, cnt)
                    TT(v, v, BANKS[done % 4][:, 0:nb * cnt].rearrange("p (b c) -> p b c", c=cnt),
                       ALU.add).then_inc(G["sd"], 1)
                    done += 1

            def gate(j):
                for h in range(2):
                    k = j * 2 + h
                    dve.wait_ge(G["py"], k + 1)
                    need(dve, G["pw"], k - 1)
                    TT(cvb[:, h], H[h][:], v_all[:, tile(at(j, h))], ALU.mult).then_inc(G["gm"], 1)
                for h in range(2):
                    dve.wait_ge(G["oT"], j * 2 + h + 1)
                    xs = res_tok[:, slot(at(j, h)), :]
                    TT(xs, xs, T[h][:].rearrange("p (s d) -> p s d", d=D), ALU.add).then_inc(G["rd"], 1)
            pairs(dve, gate)

            dve.wait_ge(G["rd"], NT)
            ln(lambda i: res_tok[:, i, :])

            def feed(j):
                for v in range(2):
                    need(dve, K["nrmT"], j * 2 + v - 1)
                    normalise(nrm[:, v], res_tok, j * 2 + v, K["nrm"])
                for v in range(2):
                    xs = x_tok[:, slot(j * 2 + v), :]
                    TT(xs, xs, res_tok[:, slot(j * 2 + v), :], ALU.add).then_inc(K["xr"], 1)
                for v in range(2):
                    t = j * 2 + v
                    dve.wait_ge(K["oT"], t + 1)
                    dve.wait_ge(K["xr"], t + 1)
                    xs = x_tok[:, slot(t), :]
                    TT(xs, xs, T[v][:].rearrange("p (s d) -> p s d", d=D), ALU.add).then_inc(K["xd"], 1)
            pairs(dve, feed)

        def attn_pool():
            nc.gpsimd.wait_ge(BS[0][1]["yo"], NBLK)
            nc.gpsimd.memset(x1p[:], 0.0).then_inc(s_bord, 1)

        def attn_act():
            act = nc.scalar

            def mix(j):
                for h in range(2):
                    k = j * 2 + h
                    act.wait_ge(G["nrmT"], k + 1)
                    need(act, G["pv"], k - 1)
                    nc.scalar.activation(hT[:, h], T[h][:], ACT.Identity, scale=col("ln1_g"),
                                         bias=col("ln1_b")).then_inc(G["hT"], 1)
                for h in range(2):
                    k = j * 2 + h
                    act.wait_ge(G["p1"], k + 1)
                    need(act, G["cv"], k - 1)
                    if isinstance(k, int) and k == 0:
                        act.wait_ge(s_bord, 1)
                    nc.scalar.activation(x1p[:, h, 1:TW + 1], H[2 * h][:], ACT.Identity,
                                         bias=col("w1_b")).then_inc(G["x1e"], 1)
                    hold(act, G["pv"], k + 1)
                    nc.scalar.activation(v_all[:, tile(at(j, h))], H[2 * h + 1][:], ACT.Silu,
                                         bias=col("v1_b")).then_inc(G["vs"], 1)
                for h in range(2):
                    k = j * 2 + h
                    act.wait_ge(G["cv"], k + 1)
                    need(act, G["pu"], k - 1)
                    nc.scalar.activation(xcb[:, h], cvb[:, h], ACT.Silu).then_inc(G["xc"], 1)
            pairs(act, mix)

            act.wait_ge(G["sd"], N_SW)

            def gate(j):
                hold(act, G["py"], j * 2)
                nc.scalar.activation(hst[:], Vt[:, bass.ds(j * TW, TW)], ACT.Copy).then_inc(G["hs"], 1)
                for h in range(2):
                    k = j * 2 + h
                    act.wait_ge(G["pw"], k + 1)
                    need(act, G["oT"], k - 1)
                    nc.scalar.activation(ob[:, h], H[2 + h][:], ACT.Identity, bias=col("w2_b")).then_inc(G["oe"], 1)
            pairs(act, gate)

            def feed(j):
                for v in range(2):
                    t = j * 2 + v
                    act.wait_ge(K["nrmT"], t + 1)
                    need(act, K["f1"], (t - 1) * 2)
                    nc.scalar.activation(hT[:, v], T[v][:], ACT.Identity, scale=col("ln2_g"),
                                         bias=col("ln2_b")).then_inc(K["hT"], 1)
                for v in range(2):
                    t = j * 2 + v
                    need(act, K["f2"], t - 1)
                    for c in range(2):
                        act.wait_ge(K["f1"], t * 2 + c + 1)
                        nc.scalar.activation(gel[:, v, c], H[2 * v + c][:], ACT.Gelu,
                                             bias=col("ff1_b", c)).then_inc(K["ge"], 1)
                for v in range(2):
                    t = j * 2 + v
                    act.wait_ge(K["f2"], t + 1)
                    need(act, K["oT"], t - 1)
                    nc.scalar.activation(ob[:, v], Y[v][:], ACT.Identity, bias=col("ff2_b")).then_inc(K["oe"], 1)
            pairs(act, feed)

        def attn_pe():
            pe = nc.tensor
            MM = nc.tensor.matmul

            def mix(j):
                for h in range(2):
                    k = j * 2 + h
                    pe.wait_ge(G["nrm"], k + 1)
                    need(pe, G["hT"], k - 1)
                    transpose_tile(T[h], lambda s: nrm[:, h, s, :], G["nrmT"])
                for h in range(2):
                    k = j * 2 + h
                    pe.wait_ge(G["hT"], k + 1)
                    need(pe, G["x1e"], k - 1)
                    MM(H[2 * h][:], wT[:, W1], hT[:, h], start=True, stop=True).then_inc(G["p1"], 1)
                    need(pe, G["vs"], k - 1)
                    MM(H[2 * h + 1][:], wT[:, V1], hT[:, h], start=True, stop=True).then_inc(G["pv"], 1)
                for h in range(2):
                    k = j * 2 + h
                    pe.wait_ge(G["xc"], k + 1)
                    need(pe, G["ue"], k - 1)
                    MM(Y[h][h * NST:(h + 1) * NST, :], wT[:, BM, 0:NST], xcb[:, h], start=True,
                       stop=True).then_inc(G["pu"], 1)
            pairs(pe, mix)

            pe.wait_ge(G["vs"], NT)
            done = 0
            pe.wait_ge(G["ue"], NT)
            for n, (l, src, _, st, cnt) in enumerate(sweeps()):
                if done:
                    pe.wait_ge(G["sd"], done)
                for b, nb in pieces(cnt):
                    MM(BANKS[done % 4][:, 0:nb * cnt].rearrange("p (b c) -> p b c", c=cnt), pwT[:, l],
                       strided(b, nb, src, st, cnt), start=True, stop=True).then_inc(G["sp"], 1)
                    done += 1
            pe.wait_ge(G["sd"], done)

            def gate(j):
                pe.wait_ge(G["hs"], j + 1)
                for h in range(2):
                    k = j * 2 + h
                    need(pe, G["gm"], k - 1)
                    hs = slice(h * NST, (h + 1) * NST)
                    MM(H[h][:], wT[hs, CM, :], hst[hs, :], start=True, stop=True).then_inc(G["py"], 1)
                for h in range(2):
                    k = j * 2 + h
                    pe.wait_ge(G["gm"], k + 1)
                    need(pe, G["oe"], k - 1)
                    MM(H[2 + h][:], wT[:, W2], cvb[:, h], start=True, stop=True).then_inc(G["pw"], 1)
                for h in range(2):
                    k = j * 2 + h
                    pe.wait_ge(G["oe"], k + 1)
                    need(pe, G["rd"], k - 1)
                    transpose_tile(T[h], lambda s: ob[:, h, s * P:(s + 1) * P], G["oT"])
            pairs(pe, gate)

            pe.wait_ge(G["rd"], NT)

            def feed(j):
                for v in range(2):
                    t = j * 2 + v
                    pe.wait_ge(K["nrm"], t + 1)
                    need(pe, K["xd"], t - 1)
                    transpose_tile(T[v], lambda s: nrm[:, v, s, :], K["nrmT"])
                for v in range(2):
                    t = j * 2 + v
                    pe.wait_ge(K["hT"], t + 1)
                    need(pe, K["ge"], (t - 1) * 2)
                    for c in range(2):
                        MM(H[2 * v + c][:], wT[:, F1 + c], hT[:, v], start=True, stop=True).then_inc(K["f1"], 1)
                for v in range(2):
                    t = j * 2 + v
                    need(pe, K["oe"], t - 1)
                    for c in range(2):
                        pe.wait_ge(K["ge"], t * 2 + c + 1)
                        ins = MM(Y[v][:], wT[:, F2 + c], gel[:, v, c], start=c == 0, stop=c == 1)
                    ins.then_inc(K["f2"], 1)
                for v in range(2):
                    t = j * 2 + v
                    pe.wait_ge(K["oe"], t + 1)
                    transpose_tile(T[v], lambda s: ob[:, v, s * P:(s + 1) * P], K["oT"])
            pairs(pe, feed)

        N_SW = sum(len(pieces(cnt)) for _, _, _, _, cnt in sweeps())

        stage = XA
        W1, V1, W2, F1, F2, BM, CM = 0, 1, 2, 3, 5, 7, 8
        loads = [(stage[:, W1], w1_w), (stage[:, V1], v1_w), (stage[:, W2], w2_w),
                 (stage[:, F1:F1 + 2], ff1_w.rearrange("(c p) d -> p c d", p=P)),
                 (stage[:, F2:F2 + 2], ff2_w.rearrange("p (c d) -> p c d", d=P)),
                 (stage[0:NST, BM], Bm), (stage[:, CM, 0:NST], Cm), (stage[:, CM, NST:P], Cm),
                 (cw[:], conv_w.rearrange("d a k -> d (a k)")), (gw[:], gate_w),
                 (gb[:], gate_b.rearrange("(a e) -> a e", a=1).to_broadcast([P, E]))]
        loads += [(rows[r:r + n, :], ap) for r, n, ap in row_loads]
        N_LD, N_BIG = len(loads), 8
        SQ = 9
        block = ctx.enter_context(nc.Block())

        def w_view(n, k):
            a = (sw1, sw2)[k] if n == 0 else (ew1, ew2)[k][n - 1]
            return a if k == 0 else a.rearrange("(c p) d -> p c d", p=P)

        @block.sync
        def _(sp):
            for dst, src in loads[:N_BIG]:
                sp.dma_start(dst, src).then_inc(s_ld, 16)
            for h in range(2):
                sl = slice(h * HS, (h + 1) * HS)
                sp.dma_start(x_tok[:, sl, :], x_view[:, sl, :]).then_inc(s_x[h], 16)
            for dst, src in loads[N_BIG:]:
                sp.dma_start(dst, src).then_inc(s_ld, 16)
            sp.wait_ge(s_zero, 2)
            for h in range(2):
                sp.dma_start(pw[h * NST:(h + 1) * NST, 0, h * NST:(h + 1) * NST], A).then_inc(s_abd, 16)
            for n in range(NE):
                if n >= 2:
                    sp.wait_ge(s_wlo, n - 1)
                for k in range(2):
                    dst = wstage[:, n % 2, k * WC:(k + 1) * WC]
                    dst = dst if k == 0 else dst.rearrange("p (c d) -> p c d", d=D)
                    sp.dma_start(dst, w_view(n, k)).then_inc(s_wst[n % 2], 16)
                if n in (1, 3):
                    h = n // 2
                    nr = HALF_BLOCKS * SB
                    sp.dma_start(xs_dram[h * nr * P:(h + 1) * nr * P, :].rearrange("(p n) d -> p n d", p=P),
                                 zrow[:, :].unsqueeze(1).to_broadcast([P, nr, P])).then_inc(s_zrow, 16)
            ffn_sp(0)
            ffn_sp(1)
            for h in range(2):
                for q in range(4):
                    sl = slice(h * HS + q * HS // 4, h * HS + (q + 1) * HS // 4)
                    sp.wait_ge(FS[1]["comb"], sl.stop)
                    sp.dma_start(out_view[:, sl, :], x_tok[:, sl, :]).then_inc(s_out, 16)
            sp.wait_ge(s_out, 16 * 8)

        @block.gpsimd
        def _(pool):
            pool.memset(pw[:, 0, :], 0.0).then_inc(s_zero, 1)
            pool.memset(zrow[:], 0.0).then_inc(s_zero, 1)
            pool.memset(ident[:], 0.0).then_inc(s_zero, 1)
            pool.memset(ones[:], 1.0).then_inc(s_zero, 1)
            pool.memset(before[:], 1.0).then_inc(s_zero, 1)
            for e in range(E):
                pool.memset(rank[:, e:e + 1], float(E - e)).then_inc(s_zero, 1)
            pool.iota(starts[:], [[BW, HALF_BLOCKS]], base=0, channel_multiplier=0,
                      allow_small_or_imprecise_dtypes=True).then_inc(s_zero, 1)
            pool.wait_ge(s_zero, 6 + E)
            nc.gpsimd.affine_select(out=ident[:], in_=ident[:], compare_op=ALU.not_equal, fill=1.0, base=0,
                                    pattern=[[-1, P]], channel_multiplier=1).then_inc(s_id, 1)
            nc.gpsimd.affine_select(out=before[:], in_=before[:], compare_op=ALU.is_gt, fill=0.0, base=0,
                                    pattern=[[1, P]], channel_multiplier=-1).then_inc(s_id, 1)
            for n in range(NE):
                pool.wait_ge(s_whi, n + 1)
                w4 = W[:, n].rearrange("p (k q) w -> p k q w", q=2)
                nc.gpsimd.tensor_tensor(w4[:, :, 1], wstage[:, n % 2].rearrange("p (k w) -> p k w", k=2),
                                        w4[:, :, 0].bitcast(F32), ALU.subtract).then_inc(s_wlo, 1)
            ffn_pool(0)
            attn_pool()
            ffn_pool(1)

        @block.scalar
        def _(act):
            for b in range(2):
                act.wait_ge(s_wT, b + 1)
                n = (4 if b == 0 else 3) * P + (0 if b == 0 else NST)
                nc.scalar.activation(wT[:, 4 * b:4 * b + 4].rearrange("p b d -> p (b d)")[:, 0:n], H[b][:, 0:n],
                                     ACT.Copy).then_inc(s_wc, 1)
            act.wait_ge(s_wT, 3)
            nc.scalar.activation(wT[:, CM], H[2][:, 0:P], ACT.Copy).then_inc(s_wc, 1)
            nc.scalar.activation(colv[:], H[2][:, P:P + n_rows], ACT.Copy).then_inc(s_wc, 1)
            nc.scalar.activation(pwT[:, 0], H[2][:, 2 * P:3 * P], ACT.Copy).then_inc(s_wc, 1)
            for l in range(1, SQ):
                act.wait_ge(s_pp, l)
                nc.scalar.activation(pw[:, l % 2], H[3][:, 0:P], ACT.Copy).then_inc(s_pw, 1)
                nc.scalar.activation(pwT[:, l], H[3][:, P:2 * P], ACT.Copy).then_inc(s_pw, 1)
            for n in range(NE):
                act.wait_ge(s_wst[n % 2], 32 * (n // 2 + 1))
                w4 = W[:, n].rearrange("p (k q) w -> p k q w", q=2)
                nc.scalar.activation(w4[:, :, 0], wstage[:, n % 2].rearrange("p (k w) -> p k w", k=2),
                                     ACT.Copy).then_inc(s_whi, 1)
                if n == 1:
                    prepare_act(0)
            softmax_act(0)
            ffn_act(0)
            attn_act()
            prepare_act(1)
            softmax_act(1)
            ffn_act(1)

        @block.vector
        def _(dve):
            ffn_dve(0)
            attn_dve()
            ffn_dve(1)
            combine(1, 0)
            combine(1, 1)

        @block.tensor
        def _(pe):
            pe.wait_ge(s_id, 2)
            pe.wait_ge(s_ld, 16 * N_LD)
            pe.wait_ge(s_abd, 32)
            TR = nc.tensor.transpose
            for b in range(7):
                ins = TR(H[b // 4][:, b % 4 * P:b % 4 * P + P], stage[:, b], ident[:])
                if b == 3:
                    ins.then_inc(s_wT, 1)
            TR(H[1][:, 3 * P:3 * P + NST], stage[0:NST, BM], ident[0:NST, 0:NST]).then_inc(s_wT, 1)
            TR(H[2][:, 0:P], stage[:, CM], ident[:])
            TR(H[2][:, P:P + n_rows], rows[0:n_rows, :], ident[0:n_rows, 0:n_rows])
            TR(H[2][:, 2 * P:3 * P], pw[:, 0], ident[:]).then_inc(s_wT, 1)
            pe.wait_ge(s_wc, 5)
            for l in range(1, SQ):
                if l > 1:
                    pe.wait_ge(s_pw, 2 * (l - 1))
                nc.tensor.matmul(H[3][:, 0:P], pwT[:, l - 1], pw[:, (l - 1) % 2], start=True, stop=True)
                nc.tensor.matmul(H[3][:, P:2 * P], pw[:, (l - 1) % 2], pwT[:, l - 1], start=True,
                                 stop=True).then_inc(s_pp, 1)
            pe.wait_ge(s_pw, 2 * (SQ - 1))
            ffn_pe(0)
            attn_pe()
            ffn_pe(1)


_INS = ['L0_attn_x', 'L0_attn_w1_w', 'L0_attn_w1_b', 'L0_attn_v1_w', 'L0_attn_v1_b', 'L0_attn_w2_w', 'L0_attn_w2_b',
        'L0_attn_conv_w', 'L0_attn_A', 'L0_attn_Bm', 'L0_attn_Cm', 'L0_attn_ln1_g', 'L0_attn_ln1_b', 'L0_attn_ln2_g',
        'L0_attn_ln2_b', 'L0_attn_ff1_w', 'L0_attn_ff1_b', 'L0_attn_ff2_w', 'L0_attn_ff2_b', 'L0_ffn_gate_w',
        'L0_ffn_gate_b', 'L0_ffn_w1', 'L0_ffn_b1', 'L0_ffn_w2', 'L0_ffn_b2', 'L0_ffn_ws1', 'L0_ffn_bs1', 'L0_ffn_ws2',
        'L0_ffn_bs2']
_OUTS = [((8, 512, 128), 'float32')]


def kernel(**inputs):
    import numpy as _np
    import concourse.bacc as _bacc
    from concourse import mybir as _mybir
    from concourse.bass_utils import run_bass_kernel_spmd as _run

    nc = _bacc.Bacc("TRN2", target_bir_lowering=False, num_devices=1)
    arrays, args = {}, []
    for name in _INS:
        a = _np.ascontiguousarray(inputs[name])
        arrays[f"in_{name}_dram"] = a
        args.append(nc.dram_tensor(f"in_{name}_dram", a.shape, _mybir.dt.from_np(a.dtype), kind="ExternalInput").ap())
    for i, (shape, dtype) in enumerate(_OUTS):
        dt = _mybir.dt.from_np(_np.dtype(dtype))
        args.append(nc.dram_tensor(f"out_{i}_dram", shape, dt, kind="ExternalOutput").ap())
    macaron_kernel(nc, *args)
    r = _run(nc, [arrays], core_ids=[0])
    got = tuple(r.results[0][f"out_{i}_dram"] for i in range(len(_OUTS)))
    return got[0]
```
